# Optimizing a Trainium2 kernel written in Bass

```python
import numpy as np
import jax
import jax.numpy as jnp

def _softmax(x, axis=-1):
    return jax.nn.softmax(x, axis=axis)

def _gelu(x):
    return jax.nn.gelu(x, approximate=True)

def _silu(x):
    return jax.nn.silu(x)

def _sigmoid(x):
    return jax.nn.sigmoid(x)

def _layernorm(x, axis=-1, eps=1e-05):
    m = jnp.mean(x, axis=axis, keepdims=True)
    v = jnp.var(x, axis=axis, keepdims=True)
    return (x - m) / jnp.sqrt(v + eps)

def _scatter_add(tgt, idx, src, axis=0):
    return tgt.at[idx].add(src)

def _segment_sum(src, seg, n):
    return jax.ops.segment_sum(src, seg, n)
kernel_name = 'mk_decoder_postln_d1_seqx_r4_5ff9c6'

def setup_inputs(seed: int=0):
    np.random.seed(seed)
    _w = jnp.asarray

    def _rec_inputs():
        import jax
        import jax.numpy as jnp
        _rk = jax.random.key(seed)
        x = 7.22e-05 + 1 * jax.random.normal(jax.random.fold_in(_rk, 1), (8, 512, 256), jnp.float32)
        _lenS = 512 - jax.random.randint(jax.random.fold_in(_rk, 7), (8,), 0, max(1, 512 // 4) + 1, jnp.int32)
        _lenS2 = 512 - jax.random.randint(jax.random.fold_in(_rk, 8), (8,), 0, max(1, 512 // 4) + 1, jnp.int32)
        _ctx_1024P = jax.random.normal(jax.random.fold_in(_rk, 11), (8, 16, 256), jnp.float32)
        _ctx_1024c = jax.random.dirichlet(jax.random.fold_in(_rk, 511), 0.3 * jnp.ones((16,), jnp.float32), (8, 512))
        _ctx_1024t = jnp.einsum('bsk,bkd->bsd', _ctx_1024c, _ctx_1024P)
        _ctx_1024t = _ctx_1024t * jax.lax.rsqrt(jnp.mean(jnp.square(_ctx_1024t)) + 1e-12) * 0.953939
        ctx_1024 = 4.13588e-05 + 0.999923 * (_ctx_1024t + 0.3 * jax.random.normal(jax.random.fold_in(_rk, 611), (8, 512, 256), jnp.float32))
        _validS = jnp.arange(512)[None, :] < _lenS[:, None]
        _validS2 = jnp.arange(512)[None, :] < _lenS2[:, None]
        _causal = jnp.tril(jnp.ones((512, 512), dtype=bool))
        mask_BxS2_bf1 = jnp.ones((8, 512), dtype=bool)
        return (x, ctx_1024, mask_BxS2_bf1)
    x, ctx_1024, mask_BxS2_bf1 = _rec_inputs()

    def _L0_attn_setup():
        import jax, jax.numpy as jnp
        import numpy as np
        NUM_HEADS = 16
        WINDOW = 64

        def _sliding_window_attn(x, wq, wk, wv, wo):
            B, S, D = x.shape
            H, W = (NUM_HEADS, WINDOW)
            Dh = D // H
            nb = S // W

            def proj(w):
                y = (x @ w.T).reshape(B, nb, W, H, Dh)
                return y.transpose(0, 3, 1, 2, 4)
            q = proj(wq)
            k = proj(wk)
            v = proj(wv)
            zpad = jnp.zeros((B, H, 1, W, Dh), dtype=x.dtype)
            kpad = jnp.concatenate([zpad, k], axis=2)
            vpad = jnp.concatenate([zpad, v], axis=2)
            k2 = jnp.concatenate([kpad[:, :, :-1], kpad[:, :, 1:]], axis=3)
            v2 = jnp.concatenate([vpad[:, :, :-1], vpad[:, :, 1:]], axis=3)
            scores = jnp.einsum('bhjqd,bhjkd->bhjqk', q, k2) / jnp.sqrt(jnp.asarray(Dh, dtype=x.dtype))
            qi = jnp.arange(W)[:, None]
            ki = jnp.arange(2 * W)[None, :]
            band = (ki >= qi + 1) & (ki <= qi + W)
            kpos_ok = (jnp.arange(nb)[:, None, None] - 1) * W + ki[None] >= 0
            mask = band[None] & kpos_ok
            neg = jnp.finfo(scores.dtype).min
            scores = jnp.where(mask[None, None], scores, neg)
            attn = jax.nn.softmax(scores, axis=-1)
            out = jnp.einsum('bhjqk,bhjkd->bhjqd', attn, v2)
            out = out.transpose(0, 2, 3, 1, 4).reshape(B, S, D)
            return out @ wo.T
        key = jax.random.key(seed)
        k1, k2, k3, k4, k5 = jax.random.split(key, 5)
        B, S, D = (2, 1024, 256)
        scale = 0.02
        return {'x': jax.random.normal(k1, (B, S, D), dtype=jnp.float32), 'wq': jax.random.normal(k2, (D, D), dtype=jnp.float32) * scale, 'wk': jax.random.normal(k3, (D, D), dtype=jnp.float32) * scale, 'wv': jax.random.normal(k4, (D, D), dtype=jnp.float32) * scale, 'wo': jax.random.normal(k5, (D, D), dtype=jnp.float32) * scale}
    _L0_attn_all = _L0_attn_setup()
    _L0_attn_in = {k: v for k, v in _L0_attn_all.items() if k in ('wq', 'wk', 'wv', 'wo')}
    del _L0_attn_all

    def _L0_xattn_setup():
        import jax, jax.numpy as jnp
        import numpy as np
        THETA = 10000.0

        def _rope_tables(T, head_dim, dtype):
            exps = jnp.arange(1, head_dim + 1, 2, dtype=jnp.float32)[:head_dim // 2] / head_dim
            w = 1.0 / THETA ** exps
            t = jnp.arange(1, T + 1, dtype=jnp.float32)
            angles = t[:, None] * w[None, :]
            return (jnp.sin(angles).astype(dtype), jnp.cos(angles).astype(dtype))

        def _rotate(x, sin, cos):
            x1 = x[..., ::2]
            x2 = x[..., 1::2]
            x1p = x1 * cos - x2 * sin
            x2p = x1 * sin + x2 * cos
            return jnp.stack((x1p, x2p), axis=-1).reshape(x.shape)
        key = jax.random.key(seed)
        B, Tq, Tkv, C = (4, 512, 512, 256)
        k1, k2, k3, k4, k5 = jax.random.split(key, 5)
        s = 1.0 / np.sqrt(C)
        return {'x_q': jax.random.normal(k1, (B, Tq, C), dtype=jnp.float32), 'x_kv': jax.random.normal(k2, (B, Tkv, C), dtype=jnp.float32), 'q_tok_mask': jnp.ones((B, Tq), dtype=bool), 'kv_tok_mask': jnp.ones((B, Tkv), dtype=bool), 'W_q': jax.random.normal(k3, (C, C), dtype=jnp.float32) * s, 'W_kv': jax.random.normal(k4, (C, 2 * C), dtype=jnp.float32) * s, 'W_c': jax.random.normal(k5, (C, C), dtype=jnp.float32) * s}
    _L0_xattn_all = _L0_xattn_setup()
    _L0_xattn_in = {k: v for k, v in _L0_xattn_all.items() if k in ('W_q', 'W_kv', 'W_c')}
    del _L0_xattn_all

    def _L0_ffn_setup():
        import jax, jax.numpy as jnp
        import numpy as np
        S, B, H, I, E = (128, 2, 256, 704, 8)
        key = jax.random.key(seed)
        ks = jax.random.split(key, 5)
        return {'hidden_states': jax.random.normal(ks[0], (S, B, H), dtype=jnp.float32), 'router_w': jax.random.normal(ks[1], (E, H), dtype=jnp.float32) * 0.02, 'gate_w': jax.random.normal(ks[2], (E, I, H), dtype=jnp.float32) * 0.02, 'up_w': jax.random.normal(ks[3], (E, I, H), dtype=jnp.float32) * 0.02, 'down_w': jax.random.normal(ks[4], (E, H, I), dtype=jnp.float32) * 0.02}
    _L0_ffn_all = _L0_ffn_setup()
    _L0_ffn_in = {k: v for k, v in _L0_ffn_all.items() if k in ('router_w', 'gate_w', 'up_w', 'down_w')}
    del _L0_ffn_all
    return {'x': x, 'ctx_1024': ctx_1024, 'mask_BxS2_bf1': mask_BxS2_bf1, 'L0_attn_wq': _L0_attn_in['wq'], 'L0_attn_wk': _L0_attn_in['wk'], 'L0_attn_wv': _L0_attn_in['wv'], 'L0_attn_wo': _L0_attn_in['wo'], 'L0_xattn_W_q': _L0_xattn_in['W_q'], 'L0_xattn_W_kv': _L0_xattn_in['W_kv'], 'L0_xattn_W_c': _L0_xattn_in['W_c'], 'L0_ffn_router_w': _L0_ffn_in['router_w'], 'L0_ffn_gate_w': _L0_ffn_in['gate_w'], 'L0_ffn_up_w': _L0_ffn_in['up_w'], 'L0_ffn_down_w': _L0_ffn_in['down_w']}

def reference(x, ctx_1024, mask_BxS2_bf1, L0_attn_wq, L0_attn_wk, L0_attn_wv, L0_attn_wo, L0_xattn_W_q, L0_xattn_W_kv, L0_xattn_W_c, L0_ffn_router_w, L0_ffn_gate_w, L0_ffn_up_w, L0_ffn_down_w):
    import jax
    import jax.numpy as jnp

    def _L0_attn_ref(x, wq, wk, wv, wo):
        import jax, jax.numpy as jnp
        import numpy as np
        NUM_HEADS = 16
        WINDOW = 64

        def _sliding_window_attn(x, wq, wk, wv, wo):
            B, S, D = x.shape
            H, W = (NUM_HEADS, WINDOW)
            Dh = D // H
            nb = S // W

            def proj(w):
                y = (x @ w.T).reshape(B, nb, W, H, Dh)
                return y.transpose(0, 3, 1, 2, 4)
            q = proj(wq)
            k = proj(wk)
            v = proj(wv)
            zpad = jnp.zeros((B, H, 1, W, Dh), dtype=x.dtype)
            kpad = jnp.concatenate([zpad, k], axis=2)
            vpad = jnp.concatenate([zpad, v], axis=2)
            k2 = jnp.concatenate([kpad[:, :, :-1], kpad[:, :, 1:]], axis=3)
            v2 = jnp.concatenate([vpad[:, :, :-1], vpad[:, :, 1:]], axis=3)
            scores = jnp.einsum('bhjqd,bhjkd->bhjqk', q, k2) / jnp.sqrt(jnp.asarray(Dh, dtype=x.dtype))
            qi = jnp.arange(W)[:, None]
            ki = jnp.arange(2 * W)[None, :]
            band = (ki >= qi + 1) & (ki <= qi + W)
            kpos_ok = (jnp.arange(nb)[:, None, None] - 1) * W + ki[None] >= 0
            mask = band[None] & kpos_ok
            neg = jnp.finfo(scores.dtype).min
            scores = jnp.where(mask[None, None], scores, neg)
            attn = jax.nn.softmax(scores, axis=-1)
            out = jnp.einsum('bhjqk,bhjkd->bhjqd', attn, v2)
            out = out.transpose(0, 2, 3, 1, 4).reshape(B, S, D)
            return out @ wo.T
        return _sliding_window_attn(x, wq, wk, wv, wo)

    def _L0_xattn_ref(x_q, x_kv, q_tok_mask, kv_tok_mask, W_q, W_kv, W_c):
        import jax, jax.numpy as jnp
        import numpy as np
        THETA = 10000.0

        def _rope_tables(T, head_dim, dtype):
            exps = jnp.arange(1, head_dim + 1, 2, dtype=jnp.float32)[:head_dim // 2] / head_dim
            w = 1.0 / THETA ** exps
            t = jnp.arange(1, T + 1, dtype=jnp.float32)
            angles = t[:, None] * w[None, :]
            return (jnp.sin(angles).astype(dtype), jnp.cos(angles).astype(dtype))

        def _rotate(x, sin, cos):
            x1 = x[..., ::2]
            x2 = x[..., 1::2]
            x1p = x1 * cos - x2 * sin
            x2p = x1 * sin + x2 * cos
            return jnp.stack((x1p, x2p), axis=-1).reshape(x.shape)
        B, Tq, C = x_q.shape
        Tkv = x_kv.shape[1]
        H = 16
        D = C // H
        q = (x_q @ W_q).reshape(B, Tq, H, D).transpose(0, 2, 1, 3)
        kv = x_kv @ W_kv
        k, v = (kv[..., :C], kv[..., C:])
        k = k.reshape(B, Tkv, H, D).transpose(0, 2, 1, 3)
        v = v.reshape(B, Tkv, H, D).transpose(0, 2, 1, 3)
        sin_q, cos_q = _rope_tables(Tq, D, x_q.dtype)
        sin_k, cos_k = _rope_tables(Tkv, D, x_q.dtype)
        q = _rotate(q, sin_q, cos_q)
        k = _rotate(k, sin_k, cos_k)
        att = jnp.einsum('bhqd,bhkd->bhqk', q, k) / jnp.sqrt(jnp.asarray(D, x_q.dtype))
        mask = (q_tok_mask[:, :, None] & kv_tok_mask[:, None, :])[:, None, :, :]
        att = jnp.where(mask, att, jnp.asarray(-1000000000.0, att.dtype))
        att = jax.nn.softmax(att, axis=-1)
        y = jnp.einsum('bhqk,bhkd->bhqd', att, v)
        y = y.transpose(0, 2, 1, 3).reshape(B, Tq, C)
        return y @ W_c

    def _L0_ffn_ref(hidden_states, router_w, gate_w, up_w, down_w):
        import jax, jax.numpy as jnp
        import numpy as np
        S, B, H, I, E = (128, 2, 256, 704, 8)
        router_logits = jnp.einsum('sbh,eh->sbe', hidden_states, router_w)
        routing_indices = jnp.argmax(router_logits, axis=-1)
        out = jnp.zeros_like(hidden_states)
        for e in range(E):
            mask = (routing_indices == e)[..., None]
            xe = jnp.where(mask, hidden_states, 0.0)
            g = jnp.einsum('sbh,ih->sbi', xe, gate_w[e])
            u = jnp.einsum('sbh,ih->sbi', xe, up_w[e])
            ye = jnp.einsum('sbi,hi->sbh', jax.nn.silu(g) * u, down_w[e])
            out = out + jnp.where(mask, ye, 0.0)
        return out
    x = _layernorm(x + _L0_attn_ref(x, L0_attn_wq, L0_attn_wk, L0_attn_wv, L0_attn_wo), axis=-1)
    x = _layernorm(x + _L0_xattn_ref(x, ctx_1024, mask_BxS2_bf1, mask_BxS2_bf1, L0_xattn_W_q, L0_xattn_W_kv, L0_xattn_W_c), axis=-1)
    x = _layernorm(x + _L0_ffn_ref(x, L0_ffn_router_w, L0_ffn_gate_w, L0_ffn_up_w, L0_ffn_down_w), axis=-1)
    return x

_drawn_inputs = setup_inputs


def setup_inputs(seed=0):
    import zlib

    import numpy as np

    out = dict(_drawn_inputs(seed))
    spreads = {}
    factors = {'L0_attn_wq': 8.0, 'L0_attn_wk': 8.0, 'L0_attn_wv': 3.862, 'L0_attn_wo': 3.907}
    for name, (base, spread) in spreads.items():
        noise = np.random.default_rng([zlib.crc32(name.encode()), seed]).standard_normal(out[name].shape)
        drawn = base * np.exp(spread * noise) if base else spread * noise
        out[name] = jnp.asarray(drawn.astype(out[name].dtype))
    for name, factor in factors.items():
        out[name] = (out[name] * factor).astype(out[name].dtype)
    return out
```

```python
from contextlib import ExitStack

import numpy as np
import concourse.bass as bass
from concourse import mybir

FP32 = mybir.dt.float32
F32R = mybir.dt.float32r
BF16 = mybir.dt.bfloat16
I32 = mybir.dt.int32
U8 = mybir.dt.uint8
U32 = mybir.dt.uint32
ALU = mybir.AluOpType
ACT = mybir.ActivationFunctionType
AX = mybir.AxisListType

P = 128
BATCH, SEQ, D = 8, 512, 256
TOKENS = BATCH * SEQ
HEADS = 16
DH = D // HEADS
T = SEQ // P
C = D // P
GROUPS, GH = 4, 4
PAIRS = HEADS // 2
STACK = 64
MAX_ROW, MASK_ROW = 3 * DH, 3 * DH + 2
WINDOW = 64
SPAN = P + WINDOW
VCOLS = DH + 1
SCALE = float(DH) ** -0.5
EPS = 1e-5
EXPERTS = 8
MASKED = -1.0e30
RING_W, RING_P = 3, 8
BIAS_HI, BIAS_LO = float(0xEE600000), float(0x000B2800)


def slot_steps(b, g, cross):
    items = T if cross else T // 2
    extras = {
        0: [("FQ", b, 4), ("FK", b, 4), ("FQ", b, 5), ("FK", b, 5), ("TO", b - 1, 2), ("SP", b + 1, 0)]
           + [("XT", b + 1, 0), ("XT", b + 1, 1)] * cross,
        1: [("FQ", b, 6), ("FK", b, 6), ("FQ", b, 7), ("FK", b, 7), ("TO", b - 1, 3),
            ("PQ", b + 1, 0), ("PK", b + 1, 0), ("PQ", b + 1, 1), ("PK", b + 1, 1)],
        2: [("TP", b - 1, 0), ("TP", b - 1, 1), ("TO", b, 0), ("PQ", b + 1, 2), ("PK", b + 1, 2),
            ("OU", b - 1, 0), ("OU", b - 1, 1), ("PQ", b + 1, 3), ("PK", b + 1, 3),
            ("LN", b - 1, 0), ("LN", b - 1, 1), ("LN", b - 1, 2)],
        3: [("TO", b, 1)] + [("RX", b - 1, 0), ("RX", b - 1, 1), ("LG", b - 1, 0)] * cross
           + [(k, b + 1, p) for p in range(4) for k in ("FQ", "FK")],
    }[g]
    at = 4 * b + g
    this, last, older = (b, g), divmod(at - 1, 4), divmod(at - 2, 4)
    n = 4 * items
    steps = [("LD", b + 1, 0), ("LR", b - 1, 0)] if g == 0 else []
    steps += [("S1", *this, i) for i in range(4)]
    steps += [("PV", *older, items - 1), ("OE", *older)]
    steps += [("MT", last[0], 2 * last[1]), ("MT", last[0], 2 * last[1] + 1)]
    done = 0
    for i in range(n):
        steps.append(("S2", *last, i))
        if i + 4 < n:
            steps.append(("S1", *this, i + 4))
        if i % 4 == 2 and i > 4:
            steps.append(("PV", *last, i // 4 - 1))
        upto = (i + 1) * len(extras) // n
        steps += extras[done:upto]
        done = upto
    steps.append(("MN", *this))
    return [s for s in steps if 0 <= s[1] < BATCH]


FREES = dict(XT="dve", PQ="act", PK="act", FQ="act", FK="dve", MT="act", TO="dve", TP="dve",
             OU="dve", RX="act", LG="dve")
BOTH = ("XT", "TP")
BUILD_STEPS = (2, 5)
NEWTON = 3
NORM_STEPS = (2, 3 + 3 * NEWTON, 0)


def events_of(s, cross):
    kind, rest = s[0], s[2:]
    if kind in FREES:
        yield "chunk_ready", rest
        if kind in BOTH:
            yield "act_took", rest
        yield FREES[kind] + "_took", rest
    if kind in ("PQ", "PK"):
        for n in range(BUILD_STEPS[cross] - 1):
            yield "pool_step", (*rest, n)
        yield "stack_built", rest
    elif kind == "SP":
        yield "dve_step", rest
        yield "split_done", rest
    elif kind == "TO":
        yield "dve_step", rest
    elif kind == "S1":
        yield "scores_ready", rest
        yield "max_taken", rest
    elif kind == "S2":
        yield "keyed_ready", rest
        yield "probs_ready", rest
    elif kind == "PV":
        yield "probs_used", rest
    elif kind == "OE":
        yield "sums_taken", rest
    elif kind == "MN":
        yield "dve_step", rest
        yield "max_placed", rest
    elif kind == "LN":
        for n in range(NORM_STEPS[rest[0]]):
            yield "dve_step", (*rest, n)
        if rest[0] == 2:
            yield "normed", rest


def plan_counts(cross):
    order, banks, in_bank, holder = {}, {}, {}, {}
    steady = 3
    for b in range(-1, BATCH + 1):
        n = 0
        for g in range(GROUPS):
            for s in slot_steps(b, g, cross):
                if s[1] == steady:
                    for label, key in events_of(s, cross):
                        order.setdefault((label, s[0]), []).append(key)
                if s[0] in FREES:
                    banks[s] = n % RING_W
                    in_bank[s] = holder.get(n % RING_W)
                    holder[n % RING_W] = s
                    n += 1
    return order, banks, in_bank


def attention_phase(nc, cross, x_rows, kvT, wq, wkv, wo, out_rows, rope=None, mask=None,
                    router=None, logits=None):
    name = "cross" if cross else "slide"
    items = T if cross else T // 2
    order, banks, in_bank = plan_counts(cross)
    rows = x_rows.rearrange("(b t p) d -> b p t d", t=T, p=P)
    rows_out = out_rows.rearrange("(b t p) d -> b p t d", t=T, p=P)
    kvT_v = kvT.rearrange("(c p) (b s) -> b p c s", p=P, s=SEQ)

    with ExitStack() as ctx:
        def sb(label, shape, dt):
            return ctx.enter_context(nc.sbuf_tensor(f"{name}_{label}", shape, dt))

        def sem(label):
            return ctx.enter_context(nc.semaphore(f"{name}_{label}"))

        w_hi = sb("w_hi", [P, C, 4 * D], F32R)
        w_lo = sb("w_lo", [P, C, 4 * D], F32R)
        ident = sb("ident", [P, P], FP32)
        ident_r = sb("ident_r", [P, P], F32R)
        kv_raw = sb("kv_raw", [P, C, SEQ], FP32)
        kv_hi = sb("kv_hi", [P, C, SEQ], F32R)
        kv_lo = sb("kv_lo", [P, C, SEQ], F32R)
        if cross:
            x_in = sb("x_in", [P, T, D], FP32)
            xT_hi = sb("xT_hi", [P, C, SEQ], F32R)
            xT_lo = sb("xT_lo", [P, C, SEQ], F32R)
        else:
            xT_hi, xT_lo = kv_hi, kv_lo
        raw = sb("raw", [P, 2, 2, D], FP32)
        qx = sb("qx", [P, 2, T, HEADS * STACK], F32R)
        kx = sb("kx", [P, 2, T, HEADS * STACK], F32R)
        qp = sb("qp", [P, HEADS, SEQ], F32R)
        kp = sb("kp", [P, PAIRS, SEQ], F32R)
        vx = sb("vx", [P, 2, T, HEADS, VCOLS], FP32)
        probs = sb("probs", [P, RING_P, SEQ], FP32)
        row_max = sb("row_max", [P, 2, GH, T], FP32)
        sums = sb("sums", [P, SEQ], FP32)
        inv = sb("inv", [P, T, GH], FP32)
        att = sb("att", [P, T, D], FP32)
        attT_hi = sb("attT_hi", [P, C, SEQ], F32R)
        attT_lo = sb("attT_lo", [P, C, SEQ], F32R)
        y = sb("y", [P, T, D], FP32)
        stats = sb("stats", [P, T, 6], FP32)
        moments = sb("moments", [P, T, 2], FP32)
        rs = sb("rs", [P, 3, T], FP32)
        if cross:
            rot = sb("rot", [P, 3, D], FP32)
            cos_m = sb("cos_m", [P, BATCH * T, DH], FP32)
            sin_m = sb("sin_m", [P, BATCH * T, DH], FP32)
            cos_sin = sb("cos_sin", [P, 2, T, DH], FP32)
            mask_u8 = sb("mask_u8", [P, BATCH * T], U8)
            valid = sb("valid", [P, BATCH * T], FP32)
            key_bias = sb("key_bias", [P, BATCH * T, 2], FP32)
            router_w = sb("router_w", [P, C, 8], FP32)
            yT = sb("yT", [P, C, SEQ], FP32)
        else:
            ident_b = sb("ident_b", [P, P], BF16)
            band = sb("band", [P, 4, SPAN], BF16)

        s1 = ctx.enter_context(nc.psum_tensor(f"{name}_s1", [P, 2, SEQ], FP32))
        s2 = ctx.enter_context(nc.psum_tensor(f"{name}_s2", [P, 2, SEQ], FP32))
        po = ctx.enter_context(nc.psum_tensor(f"{name}_po", [P, SEQ], FP32))
        wk = ctx.enter_context(nc.psum_tensor(f"{name}_wk", [P, RING_W, SEQ], FP32))

        def by_kind(label):
            return {kind: sem(f"{label}_{kind}") for lab, kind in order if lab == label}

        chunk_ready, act_took, dve_took = by_kind("chunk_ready"), by_kind("act_took"), by_kind("dve_took")
        stack_built, split_done = by_kind("stack_built"), by_kind("split_done")
        scores_ready, max_taken = by_kind("scores_ready"), by_kind("max_taken")
        keyed_ready, probs_ready = by_kind("keyed_ready"), by_kind("probs_ready")
        probs_used, sums_taken = by_kind("probs_used"), by_kind("sums_taken")
        max_placed, normed = by_kind("max_placed"), by_kind("normed")
        dve_step, pool_step = by_kind("dve_step"), by_kind("pool_step")
        prep_step, prep_pool = sem("prep_step"), sem("prep_pool")
        w_loaded, consts_loaded = sem("w_loaded"), sem("consts_loaded")
        kv_loaded, x_loaded, res_loaded, y_free = (
            sem("kv_loaded"), sem("x_loaded"), sem("res_loaded"), sem("y_free"))
        consts_made, w_split, po_cleared = sem("consts_made"), sem("w_split"), sem("po_cleared")
        POOL_CONSTS = 2 if cross else 3

        pool_engine, sync_engine = nc.gpsimd, nc.sync
        LOOP_FROM, LOOP_PERIOD = 1, 2

        def run_batches(eng, part):
            for b in (-1, 0):
                for g in range(GROUPS):
                    for s in slot_steps(b, g, cross):
                        part(s, None)
            with eng.Fori(0, (BATCH - 2) // LOOP_PERIOD) as it:
                for b in range(LOOP_FROM, LOOP_FROM + LOOP_PERIOD):
                    for g in range(GROUPS):
                        for s in slot_steps(b, g, cross):
                            part(s, it)
            for b in (BATCH - 1, BATCH):
                for g in range(GROUPS):
                    for s in slot_steps(b, g, cross):
                        part(s, None)

        def wait_for(eng, semaphores, label, it, kind, b, *rest, alone=False):
            keys = order[label, kind]
            if (label, kind) == ("chunk_ready", "RX"):
                b += 1
            wait_times(eng, semaphores[kind], it, b, len(keys), keys.index(rest) + 1, alone)

        def wait_times(eng, semaphore, it, b, per_batch, base, alone=False):
            n = per_batch * b + base
            if it is None:
                if b >= 0:
                    eng.wait_ge(semaphore, n)
            else:
                assert n > 0
                count = it * (per_batch * LOOP_PERIOD) + n
                if alone or eng is pool_engine or eng is sync_engine:
                    count = eng.to_reg(count)
                    eng.wait_ge(consts_made, 1)
                eng.wait_ge(semaphore, count)

        def batch_at(it, b):
            return b if it is None else it * LOOP_PERIOD + b

        def by_head(stack):
            return stack.rearrange("p t (h r) -> p t h r", r=STACK)

        def ring_before(s, back):
            kind, b, g, i = s
            n = (GROUPS * b + g) * items * GH + i - back
            if n < 0:
                return None
            at, i = divmod(n, items * GH)
            return (kind, at // GROUPS, at % GROUPS, i)

        block = ctx.enter_context(nc.Block())

        @block.tensor
        def _(pe):
            def free_bank(s, it):
                held = in_bank[s]
                if held is not None:
                    if FREES[held[0]] == "act":
                        wait_for(pe, act_took, "act_took", it, *held)
                    else:
                        wait_for(pe, dve_took, "dve_took", it, *held)
                return wk[:, banks[s], :]

            def product3(out, a_hi, a_lo, w0, w1, t):
                for c in range(C):
                    tok = slice(t * P, (t + 1) * P)
                    pe.matmul(out, a_hi[:, c, tok], w_hi[:, c, w0:w1], start=(c == 0), stop=False)
                    pe.matmul(out, a_hi[:, c, tok], w_lo[:, c, w0:w1], start=False, stop=False)
                    last = pe.matmul(out, a_lo[:, c, tok], w_hi[:, c, w0:w1], start=False, stop=(c == C - 1))
                return last

            def part(s, it):
                kind, b = s[0], s[1]
                if kind in FREES:
                    i = s[2]
                    bank = free_bank(s, it)
                    bank_r = bank.bitcast(F32R)
                if kind == "XT":
                    if i == 0:
                        wait_times(pe, x_loaded, it, b, 16, 16)
                    for t in range(T):
                        last = pe.transpose(bank[:, t * P:(t + 1) * P], x_in[:, t, i * P:(i + 1) * P], ident[:])
                elif kind == "PQ":
                    if i == 0:
                        if cross:
                            wait_for(pe, dve_took, "dve_took", it, "XT", b, C - 1)
                        wait_for(pe, split_done, "split_done", it, "SP", b, 0)
                    last = product3(bank[:, 0:D], xT_hi, xT_lo, 0, D, i)
                elif kind == "PK":
                    last = product3(bank[:, 0:2 * D], kv_hi, kv_lo, D, 3 * D, i)
                elif kind in ("FQ", "FK", "MT"):
                    if kind == "MT":
                        if i % 2 == 0:
                            wait_for(pe, max_placed, "max_placed", it, "MN", b, i // 2)
                    else:
                        wait_for(pe, stack_built, "stack_built", it, "PK", b, T - 1)
                    stacks = kx if kind == "FK" else qx
                    for t in range(T):
                        last = pe.transpose(bank_r[:, t * P:(t + 1) * P],
                                            stacks[:, b % 2, t, i * P:(i + 1) * P], ident_r[:])
                elif kind == "TO":
                    wait_for(pe, sums_taken, "sums_taken", it, "OE", b, i)
                    for t in range(T):
                        last = pe.transpose(bank[:, t * P:(t + 1) * P], sums[:, t * P:(t + 1) * P], ident[:])
                elif kind == "TP":
                    wait_for(pe, dve_took, "dve_took", it, "TO", b, GROUPS - 1)
                    for t in range(T):
                        last = pe.transpose(bank[:, t * P:(t + 1) * P], att[:, t, i * P:(i + 1) * P], ident[:])
                elif kind == "OU":
                    wait_for(pe, dve_took, "dve_took", it, "TP", b, C - 1)
                    for half in range(2):
                        last = product3(bank[:, half * D:(half + 1) * D], attT_hi, attT_lo,
                                        3 * D, 4 * D, 2 * i + half)
                elif kind == "RX":
                    wait_for(pe, normed, "normed", it, "LN", b, 2)
                    for t in range(T):
                        last = pe.transpose(bank[:, t * P:(t + 1) * P], y[:, t, i * P:(i + 1) * P], ident[:])
                elif kind == "LG":
                    wait_for(pe, act_took, "act_took", it, "RX", b, C - 1)
                    for t in range(T):
                        for c in range(C):
                            last = pe.matmul(bank[:, 8 * t:8 * t + 8], yT[:, c, t * P:(t + 1) * P],
                                             router_w[:, c, :], start=(c == 0), stop=(c == C - 1))
                elif kind == "S1":
                    g, i = s[2], s[3]
                    c, j = divmod(i, items)
                    h = GH * g + c
                    if j == 0:
                        wait_for(pe, act_took, "act_took", it, "FQ", b, h // 2)
                        wait_for(pe, dve_took, "dve_took", it, "FK", b, h // 2)
                    before = ring_before(s, 2)
                    if before:
                        wait_for(pe, max_taken, "max_taken", it, *before)
                    out = s1[:, i % 2, :]
                    if cross:
                        last = pe.matmul(out, qp[:, h, j * P:(j + 1) * P], kp[:, h // 2, :],
                                         start=True, stop=True)
                    else:
                        for half in range(2):
                            t = 2 * j + half
                            at = 3 * WINDOW if t == 1 else 2 * P * half
                            keys = max(0, (t - 1) * P)
                            seen = at + (0 if t == 0 else WINDOW)
                            pe.matmul(out[:, at:at + 2 * P], qp[:, h, t * P:(t + 1) * P],
                                      kp[:, h // 2, keys:keys + 2 * P], start=True, stop=False)
                            last = pe.matmul(out[:, seen:seen + SPAN], ident_b[:],
                                             band[:, 1 if t == 0 else 0, :], start=False, stop=True)
                    last.then_inc(scores_ready[kind], 1)
                    return
                elif kind == "S2":
                    g, i = s[2], s[3]
                    j, c = divmod(i, GH)
                    h = GH * g + c
                    if i == 0:
                        wait_for(pe, act_took, "act_took", it, "MT", b, 2 * g + 1)
                    before = ring_before(s, 2)
                    if before:
                        wait_for(pe, probs_ready, "probs_ready", it, *before)
                    out = s2[:, i % 2, :]
                    if cross:
                        last = pe.matmul(out, kp[:, h // 2, j * P:(j + 1) * P], qp[:, h, :],
                                         start=True, stop=True)
                    else:
                        for half in range(2):
                            t = 2 * j + half
                            at = 3 * WINDOW if t == 3 else 2 * P * half
                            queries = min(t * P, SEQ - 2 * P)
                            seen = at + (WINDOW if t == T - 1 else 0)
                            pe.matmul(out[:, at:at + 2 * P], kp[:, h // 2, t * P:(t + 1) * P],
                                      qp[:, h, queries:queries + 2 * P], start=True, stop=False)
                            last = pe.matmul(out[:, seen:seen + SPAN], ident_b[:],
                                             band[:, 3 if t == T - 1 else 2, :], start=False, stop=True)
                    last.then_inc(keyed_ready[kind], 1)
                    return
                elif kind == "PV":
                    g, j = s[2], s[3]
                    wait_for(pe, probs_ready, "probs_ready", it, "S2", b, g, GH * j + GH - 1)
                    if j == 0:
                        wait_for(pe, act_took, "act_took", it, "PK", b, T - 1)
                        gb, gg = divmod(4 * b + g - 1, GROUPS)
                        wait_for(pe, sums_taken, "sums_taken", it, "OE", gb, gg)
                    for half in range(1 if cross else 2):
                        t = j if cross else 2 * j + half
                        for c in range(GH):
                            slot = (items * GH * g + GH * j + c) % RING_P
                            if cross:
                                out, p = po[32 * c:32 * c + VCOLS, :], probs[:, slot, :]
                            else:
                                q0 = min(t * P, SEQ - SPAN)
                                out = po[32 * c:32 * c + VCOLS, q0:q0 + SPAN]
                                p = probs[:, slot, half * SPAN:(half + 1) * SPAN]
                            last = pe.matmul(out, vx[:, b % 2, t, GH * g + c, :], p, start=(t == 0),
                                             stop=(t == T - 1), tile_position=(0, 32 * c),
                                             skip_group_check=True)
                    last.then_inc(probs_used[kind], 1)
                    return
                else:
                    return
                last.then_inc(chunk_ready[kind], 1)

            pe.wait_ge(consts_made, 1)
            pe.wait_ge(w_split, 1)
            pe.wait_ge(po_cleared, 1)
            run_batches(pe, part)

        @block.scalar
        def _(act):
            def part(s, it):
                kind, b = s[0], s[1]
                if kind in FREES:
                    i = s[2]
                    bank = wk[:, banks[s], :]
                    if kind in BOTH or FREES[kind] == "act":
                        wait_for(act, chunk_ready, "chunk_ready", it, *s)
                if kind == "XT":
                    act.activation(xT_hi[:, i, :], bank, ACT.Copy).then_inc(act_took[kind], 1)
                elif kind == "PQ" or kind == "PK":
                    tb, tt = divmod(T * b + i - 2, T)
                    wait_for(act, stack_built, "stack_built", it, kind, tb, tt)
                    if kind == "PK":
                        act.activation(vx[:, b % 2, i, :, 0:DH],
                                       bank[:, D:2 * D].rearrange("p (h d) -> p h d", d=DH), ACT.Copy)
                    act.activation(raw[:, i % 2, int(kind == "PK"), :], bank[:, 0:D], ACT.Copy)\
                       .then_inc(act_took[kind], 1)
                elif kind == "FQ" or kind == "MT":
                    r = 32 if kind == "MT" else 0
                    act.activation(qp[r:64, 2 * i, :], bank[r:64, :], ACT.Copy)
                    act.activation(qp[64 + r:P, 2 * i + 1, :], bank[64 + r:P, :], ACT.Copy)\
                       .then_inc(act_took[kind], 1)
                elif kind == "TP":
                    act.activation(attT_hi[:, i, :], bank, ACT.Copy).then_inc(act_took[kind], 1)
                elif kind == "RX":
                    act.activation(yT[:, i, :], bank, ACT.Copy).then_inc(act_took[kind], 1)
                elif kind == "S2":
                    wait_for(act, keyed_ready, "keyed_ready", it, *s)
                    g, i = s[2], s[3]
                    before = ring_before(s, RING_P)
                    if before:
                        wait_for(act, probs_used, "probs_used", it, "PV", before[1], before[2], before[3] // GH)
                    slot = (items * GH * g + i) % RING_P
                    if cross:
                        out, in_ = probs[:, slot, :], s2[:, i % 2, :]
                    else:
                        out = probs[:, slot, 0:2 * SPAN].rearrange("p (a n) -> p a n", a=2)
                        in_ = s2[:, i % 2, :].rearrange("p (a n) -> p a n", a=2)[:, :, 0:SPAN]
                    act.activation(out, in_, ACT.Exp, scale=SCALE).then_inc(probs_ready[kind], 1)
                elif kind == "OE":
                    g = s[2]
                    wait_for(act, probs_used, "probs_used", it, "PV", b, g, items - 1)
                    gb, gg = divmod(GROUPS * b + g - 1, GROUPS)
                    wait_for(act, chunk_ready, "chunk_ready", it, "TO", gb, gg)
                    act.activation(sums[:], po[:], ACT.Copy).then_inc(sums_taken[kind], 1)

            act.wait_ge(consts_made, 1)
            act.wait_ge(w_split, 1)
            run_batches(act, part)

        @block.vector
        def _(dve):
            stage = probs[:, 0:4, :].rearrange("p (c x) n -> p c (x n)", c=C)
            dve.wait_ge(w_loaded, 48)
            dve.tensor_copy(w_hi[:], stage).then_inc(prep_step, 1)
            dve.wait_ge(prep_step, 1)
            dve.tensor_tensor(w_lo[:], stage, w_hi[:].bitcast(FP32), ALU.subtract).then_inc(w_split, 1)
            dve.memset(po[:], 0.0).then_inc(po_cleared, 1)
            dve.wait_ge(prep_pool, POOL_CONSTS)
            if cross:
                dve.wait_ge(consts_loaded, 48)
                dve.tensor_copy(valid[:], mask_u8[:]).then_inc(prep_step, 1)
                dve.wait_ge(prep_step, 2)
                for part_, bias in enumerate((BIAS_HI, BIAS_LO)):
                    dve.tensor_scalar(key_bias[:, :, part_:part_ + 1], valid[:].unsqueeze(2), bias, -bias,
                                      ALU.mult, ALU.add)
                for k, table in enumerate((cos_m, sin_m)):
                    for b in range(BATCH):
                        keep = valid[:, T * b:T * b + T].unsqueeze(2).to_broadcast([P, T, DH])
                        dve.tensor_tensor(table[:, T * b:T * b + T, :], cos_sin[:, k, :, :], keep, ALU.mult)
            else:
                dve.tensor_copy(ident_b[:], ident[:])
            dve.tensor_copy(ident_r[:], ident[:]).then_inc(consts_made, 1)

            def part(s, it):
                kind, b = s[0], s[1]
                if kind in FREES:
                    i = s[2]
                    bank = wk[:, banks[s], :]
                    if kind in BOTH:
                        wait_for(dve, act_took, "act_took", it, *s)
                    elif FREES[kind] == "dve":
                        wait_for(dve, chunk_ready, "chunk_ready", it, *s)
                if kind == "XT":
                    dve.tensor_tensor(xT_lo[:, i, :], bank, xT_hi[:, i, :].bitcast(FP32), ALU.subtract)\
                       .then_inc(dve_took[kind], 1)
                elif kind == "SP":
                    wait_times(dve, kv_loaded, it, b, 16, 16)
                    wait_for(dve, chunk_ready, "chunk_ready", it, "PK", b - 1, T - 1)
                    dve.tensor_copy(kv_hi[:], kv_raw[:]).then_inc(dve_step[kind], 1)
                    wait_for(dve, dve_step, "dve_step", it, *s)
                    dve.tensor_tensor(kv_lo[:], kv_raw[:], kv_hi[:].bitcast(FP32), ALU.subtract)\
                       .then_inc(split_done[kind], 1)
                elif kind == "FK":
                    dve.tensor_copy(kp[:, i, :], bank).then_inc(dve_took[kind], 1)
                elif kind == "TO":
                    v = bank.rearrange("p (t c r) -> p t c r", t=T, c=GH)
                    gb, gg = divmod(GROUPS * b + i - 1, GROUPS)
                    wait_for(dve, dve_took, "dve_took", it, "TO", gb, gg)
                    dve.reciprocal(inv[:].unsqueeze(3), v[:, :, :, DH:DH + 1]).then_inc(dve_step[kind], 1)
                    wait_for(dve, dve_step, "dve_step", it, *s)
                    out = att[:, :, DH * GH * i:DH * GH * (i + 1)].rearrange("p t (c d) -> p t c d", c=GH)
                    dve.tensor_tensor(out, v[:, :, :, 0:DH], inv[:].unsqueeze(3).to_broadcast([P, T, GH, DH]),
                                      ALU.mult).then_inc(dve_took[kind], 1)
                elif kind == "TP":
                    dve.tensor_tensor(attT_lo[:, i, :], bank, attT_hi[:, i, :].bitcast(FP32), ALU.subtract)\
                       .then_inc(dve_took[kind], 1)
                elif kind == "OU":
                    if i == 0:
                        wait_times(dve, res_loaded, it, b, 16, 16)
                    out = y[:, 2 * i:2 * i + 2, :]
                    dve.tensor_tensor(out, bank.rearrange("p (t d) -> p t d", t=2), out, ALU.add)\
                       .then_inc(dve_took[kind], 1)
                elif kind == "LG":
                    dve.tensor_copy(logits[:, bass.ds(batch_at(it, b) * T, T), :],
                                    bank[:, 0:8 * T].rearrange("p (t e) -> p t e", e=8)).then_inc(dve_took[kind], 1)
                elif kind == "S1":
                    g, i = s[2], s[3]
                    c, j = divmod(i, items)
                    wait_for(dve, scores_ready, "scores_ready", it, *s)
                    if cross:
                        dve.reduce_max(row_max[:, g % 2, c, j:j + 1], s1[:, i % 2, :], axis=AX.X)\
                           .then_inc(max_taken[kind], 1)
                    else:
                        seen = s1[:, i % 2, :].rearrange("p (a n) -> p a n", a=2)
                        seen = seen[:, :, 0:SPAN] if j == 0 else seen[:, :, WINDOW:WINDOW + SPAN]
                        dve.reduce_max(row_max[:, g % 2, c, 2 * j:2 * j + 2], seen, axis=AX.X)\
                           .then_inc(max_taken[kind], 1)
                elif kind == "MN":
                    g = s[2]
                    wait_for(dve, max_taken, "max_taken", it, "S1", b, g, items * GH - 1)
                    rows_ = by_head(qx[:, b % 2])[:, :, GH * g:GH * g + GH, MAX_ROW:MAX_ROW + 2]
                    m = row_max[:, g % 2].rearrange("p c t -> p t c").unsqueeze(3)
                    dve.tensor_scalar(rows_[:, :, :, 0:1], m, -1.0, None, ALU.mult).then_inc(dve_step[kind], 1)
                    wait_for(dve, dve_step, "dve_step", it, *s)
                    dve.scalar_tensor_tensor(rows_[:, :, :, 1:2], m, -1.0, rows_[:, :, :, 0:1].bitcast(FP32),
                                             ALU.mult, ALU.subtract).then_inc(max_placed[kind], 1)
                elif kind == "LN":
                    k = s[2]
                    if k == 0:
                        wait_for(dve, dve_took, "dve_took", it, "OU", b, 1)
                        for t in range(T):
                            last = dve.bn_stats(stats[:, t, :], y[:, t, :])
                        last.then_inc(dve_step[kind], 1)
                        wait_for(dve, dve_step, "dve_step", it, *s, 0, alone=True)
                        for t in range(T):
                            last = dve.bn_aggr(moments[:, t, :], stats[:, t, :])
                        last.then_inc(dve_step[kind], 1)
                    elif k == 1:
                        var, root, scratch = rs[:, 0, :], rs[:, 1, :], rs[:, 2, :]
                        wait_for(dve, dve_step, "dve_step", it, "LN", b, 0, 1)
                        dve.tensor_scalar(var.unsqueeze(2), moments[:, :, 1:2], EPS, None, ALU.add).then_inc(dve_step[kind], 1)
                        wait_for(dve, dve_step, "dve_step", it, *s, 0)
                        dve.tensor_scalar(scratch.bitcast(I32), var.bitcast(I32), 1, None, ALU.arith_shift_right)\
                           .then_inc(dve_step[kind], 1)
                        wait_for(dve, dve_step, "dve_step", it, *s, 1)
                        dve.tensor_scalar(root.bitcast(I32), scratch.bitcast(I32), -1.0, float(0x5F3759DF),
                                          ALU.mult, ALU.add).then_inc(dve_step[kind], 1)
                        for n in range(NEWTON):
                            wait_for(dve, dve_step, "dve_step", it, *s, 2 + 3 * n)
                            dve.tensor_tensor(scratch, root, root, ALU.mult).then_inc(dve_step[kind], 1)
                            wait_for(dve, dve_step, "dve_step", it, *s, 3 + 3 * n)
                            dve.scalar_tensor_tensor(scratch, scratch, -0.5, var, ALU.mult, ALU.mult)\
                               .then_inc(dve_step[kind], 1)
                            wait_for(dve, dve_step, "dve_step", it, *s, 4 + 3 * n)
                            dve.scalar_tensor_tensor(root, scratch, 1.5, root, ALU.add, ALU.mult)\
                               .then_inc(dve_step[kind], 1)
                    else:
                        wait_for(dve, dve_step, "dve_step", it, "LN", b, 1, NORM_STEPS[1] - 1)
                        for t in range(T):
                            last = dve.tensor_scalar(y[:, t, :], y[:, t, :], moments[:, t, 0:1], rs[:, 1, t:t + 1],
                                                     ALU.subtract, ALU.mult)
                        last.then_inc(normed[kind], 1)

            run_batches(dve, part)

        @block.gpsimd
        def _(pool):
            pool.memset(ident[:], 0.0)
            pool.memset(qx[:].bitcast(FP32), 0.0)
            pool.memset(kx[:].bitcast(FP32), 0.0)
            pool.memset(qp[:].bitcast(FP32), 0.0)
            last = pool.memset(vx[:], 1.0)
            if not cross:
                last = pool.memset(band[:], 0.0)
            last.then_inc(prep_pool, 1)
            pool.wait_ge(prep_pool, 1)
            done = pool.affine_select(out=ident[:], in_=ident[:], compare_op=ALU.not_equal, fill=1.0, base=0,
                                      pattern=[[-1, P]], channel_multiplier=1)
            for half in range(2):
                pool.memset(by_head(kx[:, half])[:, :, :, MAX_ROW:MAX_ROW + 2].bitcast(FP32), 1.0)
            if not cross:
                edges = ((-1, -1, 1), (0, 0, -1), (0, -1, 1), (-WINDOW, -1, 1))
                others = ((WINDOW, 1, -1), (WINDOW - 1, -1, 1), (WINDOW - 1, 1, -1), (P - 1, 1, -1))
                for n in range(4):
                    base, row, col = edges[n]
                    if n == 1:
                        base, row, col = 0, 1, -1
                    done = pool.affine_select(out=band[:, n, :], in_=band[:, n, :], compare_op=ALU.is_ge, fill=MASKED,
                                              base=base, pattern=[[col, SPAN]], channel_multiplier=row)
                done.then_inc(prep_pool, 1)
                pool.wait_ge(prep_pool, 2)
                for n in range(4):
                    base, row, col = others[n]
                    done = pool.affine_select(out=band[:, n, :], in_=band[:, n, :], compare_op=ALU.is_ge, fill=MASKED,
                                              base=base, pattern=[[col, SPAN]], channel_multiplier=row)
            done.then_inc(prep_pool, 1)
            pool.wait_ge(prep_pool, POOL_CONSTS)
            pool.wait_ge(consts_made, 1)

            def part(s, it):
                kind, b = s[0], s[1]
                if kind not in ("PQ", "PK"):
                    return
                t, is_key = s[2], kind == "PK"
                wait_for(pool, act_took, "act_took", it, *s)
                stack = by_head((kx if is_key else qx)[:, b % 2])
                at = batch_at(it, b) * T
                if t == 0:
                    if is_key and cross:
                        pool.tensor_copy(stack[:, :, :, MASK_ROW:MASK_ROW + 2],
                                         key_bias[:, bass.ds(at, T), :].unsqueeze(2).to_broadcast([P, T, HEADS, 2]))
                    if not is_key:
                        pool.memset(stack[:, :, :, MAX_ROW:MAX_ROW + 2].bitcast(FP32), 0.0)
                        if cross:
                            keep = valid[:, bass.ds(at, T)].unsqueeze(2).unsqueeze(3)
                            pool.tensor_copy(stack[:, :, :, MASK_ROW:MASK_ROW + 2],
                                             keep.to_broadcast([P, T, HEADS, 2]))
                source = raw[:, t % 2, int(is_key), :]
                out = stack[:, t]
                heads = source.rearrange("p (h d) -> p h d", d=DH)
                n = 0
                if cross:
                    def table(m):
                        return m[:, bass.ds(at + t, 1), :].to_broadcast([P, HEADS, DH])
                    pairs = source.rearrange("p (h i two) -> p h i two", h=HEADS, two=2)
                    if True:
                        tb, tt = divmod(T * b + t - (0 if is_key else 1), T)
                        wait_for(pool, stack_built, "stack_built", it, "PQ" if is_key else "PK", tb, tt)
                    pool.tensor_tensor(rot[:, 0, :].rearrange("p (h d) -> p h d", d=DH), heads, table(cos_m), ALU.mult)\
                        .then_inc(pool_step[kind], 1)
                    pool.tensor_tensor(rot[:, 1, :].rearrange("p (h i two) -> p h i two", h=HEADS, two=2),
                                       pairs[:, :, :, ::-1],
                                       table(sin_m).rearrange("p h (i two) -> p h i two", two=2), ALU.mult)\
                        .then_inc(pool_step[kind], 1)
                    wait_for(pool, pool_step, "pool_step", it, *s, 1)
                    pool.tensor_tensor(rot[:, 2, :], rot[:, 0, :], rot[:, 1, :], ALU.add).then_inc(pool_step[kind], 1)
                    wait_for(pool, pool_step, "pool_step", it, *s, 2)
                    heads = rot[:, 2, :].rearrange("p (h d) -> p h d", d=DH)
                    n = 3
                a, z, low = (0, 2, 1) if is_key else (0, 1, 2)
                both = out[:, :, 0:3 * DH].rearrange("p h (k d) -> p h k d", k=3)
                pool.tensor_copy(both[:, :, a:z + 1:z - a, :], heads.unsqueeze(2).to_broadcast([P, HEADS, 2, DH]))\
                    .then_inc(pool_step[kind], 1)
                wait_for(pool, pool_step, "pool_step", it, *s, n)
                pool.tensor_tensor(both[:, :, low, :], heads, both[:, :, 0, :].bitcast(FP32), ALU.subtract)\
                    .then_inc(stack_built[kind], 1)

            run_batches(pool, part)

        @block.sync
        def _(sp):
            sp.sem_inc(y_free, 16)
            if cross:
                sp.sem_inc(chunk_ready["RX"], C)
            stage = probs[:, 0:4, :].rearrange("p (c x) n -> p c (x n)", c=C)
            sp.dma_start(stage[:, :, 0:D], wq.rearrange("(c p) n -> p c n", p=P)).then_inc(w_loaded, 16)
            sp.dma_start(stage[:, :, D:3 * D], wkv.rearrange("(c p) n -> p c n", p=P)).then_inc(w_loaded, 16)
            sp.dma_start(stage[:, :, 3 * D:], wo.rearrange("(c p) n -> p c n", p=P)).then_inc(w_loaded, 16)
            if cross:
                sp.dma_start(mask_u8[:], mask).then_inc(consts_loaded, 16)
                sp.dma_start(cos_sin[:], rope).then_inc(consts_loaded, 16)
                sp.dma_start(router_w[:], router.rearrange("(c p) e -> p c e", p=P)).then_inc(consts_loaded, 16)

            def part(s, it):
                kind, b = s[0], s[1]
                if kind == "LD":
                    wait_for(sp, split_done, "split_done", it, "SP", b - 1, 0)
                    sp.dma_start(kv_raw[:], at_batch(kvT_v, it, b)).then_inc(kv_loaded, 16)
                    if cross:
                        wait_for(sp, chunk_ready, "chunk_ready", it, "XT", b - 1, C - 1)
                        sp.dma_start(x_in[:], at_batch(rows, it, b)).then_inc(x_loaded, 16)
                elif kind == "LR":
                    wait_times(sp, y_free, it, b, 16, 16)
                    if cross:
                        wait_for(sp, chunk_ready, "chunk_ready", it, "RX", b - 1, C - 1)
                    sp.dma_start(y[:], at_batch(rows, it, b)).then_inc(res_loaded, 16)
                elif kind == "LN" and s[2] == 2:
                    wait_for(sp, normed, "normed", it, *s)
                    sp.dma_start(at_batch(rows_out, it, b), y[:]).then_inc(y_free, 16)

            def at_batch(view, it, b):
                return view[b] if it is None else view[bass.ds(it * LOOP_PERIOD + b, 1)].squeeze(0)

            run_batches(sp, part)
            sp.wait_ge(y_free, 16 * (BATCH + 1))


def expert_phase(nc, x2, logits, gate_w, up_w, down_w, out):
    E, HID = EXPERTS, gate_w.shape[2]
    TT = BATCH * T
    TILES = TT + E - 1
    HALF = HID // 2
    HC = -(-HID // P)
    LAST = HID - (HC - 1) * P
    SHIFT = P.bit_length() - 1
    SKIP = 2.0 * TOKENS
    PERIOD = 4
    NORM = 2 + 3 + 3 * NEWTON

    with ExitStack() as ctx:
        def sb(label, shape, dt):
            return ctx.enter_context(nc.sbuf_tensor(f"moe_{label}", shape, dt))

        def sem(label):
            return ctx.enter_context(nc.semaphore(f"moe_{label}"))

        def pb(label, shape):
            return ctx.enter_context(nc.psum_tensor(f"moe_{label}", shape, FP32))

        wg = sb("wg", [P, E, C, HID], FP32)
        wu = sb("wu", [P, E, C, HID], FP32)
        wd = sb("wd", [P, E, HC, D], FP32)
        ident = sb("ident", [P, P], FP32)
        best = sb("best", [P, TT], FP32)
        pick = sb("pick", [P, TT, E], FP32)
        onehot = sb("onehot", [P, TT, E], BF16)
        before = sb("before", [P, P], BF16)
        ones = sb("ones", [P, P], BF16)
        descend = sb("descend", [P, E], FP32)
        upto = sb("upto", [P, E, E], FP32)
        count = sb("count", [P, E], FP32)
        count_i = sb("count_i", [P, E], I32)
        ntiles = sb("ntiles", [P, E], FP32)
        running = sb("running", [P, E, E], FP32)
        ends = sb("ends", [P, E], FP32)
        starts = sb("starts", [P, E], FP32)
        slot = sb("slot", [P, TT], FP32)
        slot_i = sb("slot_i", [P, 3, TT], I32)
        slot_f = sb("slot_f", [P, 2, TT], FP32)
        iota_i = sb("iota_i", [P, P], I32)
        iota_f = sb("iota_f", [P, P], FP32)
        row_i = sb("row_i", [P, 1], I32)
        row_f = sb("row_f", [P, 1], FP32)
        behind = sb("behind", [P, TILES, E], FP32)
        tile_expert = sb("tile_expert", [P, TILES], FP32)
        tile_expert_i = sb("tile_expert_i", [P, TILES], I32)
        place = sb("place", [P, TT, P], BF16)
        marks = sb("marks", [P, TT, 3, TILES], BF16)
        found = sb("found", [P, 3, TILES], FP32)
        take_f = sb("take_f", [P, 2, TILES], FP32)
        take = sb("take", [P, 2, TILES], U32)
        now = sb("now", [P, 2, 2], U32)
        xg = sb("xg", [P, PERIOD, D], FP32)
        xT = sb("xT", [P, 2, C, P], FP32)
        act_g = sb("act_g", [P, 2, HID], FP32)
        h = sb("h", [P, 2, HID], FP32)
        hT = sb("hT", [P, 2, HC, P], FP32)
        y = sb("y", [P, PERIOD, D], FP32)
        stats = sb("stats", [P, 6], FP32)
        moments = sb("moments", [P, 2], FP32)
        rs = sb("rs", [P, 3], FP32)

        g_ps, u_ps, t_ps = pb("g", [P, 2, SEQ]), pb("u", [P, 2, SEQ]), pb("t", [P, 2, SEQ])
        x_ps, d_ps = pb("x", [P, SEQ]), pb("d", [P, SEQ])

        consts, route_step, ranked = sem("consts"), sem("route_step"), sem("ranked")
        placed, inverted, routed = sem("placed"), sem("inverted"), sem("routed")
        expert_loaded = [sem(f"expert_loaded{e}") for e in range(E)]
        experts_ready = sem("experts_ready")
        gathered = [sem(f"gathered{n}") for n in range(PERIOD)]
        scattered = [sem(f"scattered{n}") for n in range(PERIOD)]
        index_copied, xT_psum, xT_ready = sem("index_copied"), sem("xT_psum"), sem("xT_ready")
        gate_ready, up_ready, gate_act = sem("gate_ready"), sem("up_ready"), sem("gate_act")
        h_ready, hT_psum, hT_low, hT_high = sem("h_ready"), sem("hT_psum"), sem("hT_low"), sem("hT_high")
        down_ready, summed, norm_step, y_ready = sem("down_ready"), sem("summed"), sem("norm_step"), sem("y_ready")

        def run_slots(eng, part):
            first = PERIOD + 1
            turns = (TILES - 3 - first) // PERIOD
            behind_loop = first + turns * PERIOD
            for s in range(-3, first):
                part(s, None)
            with eng.Fori(0, turns) as it:
                for s in range(first, first + PERIOD):
                    part(s, it)
            for s in range(behind_loop, TILES + 2):
                part(s, None)

        def wait_n(eng, semaphore, it, s, base=1, per_tile=1, alone=False):
            n = per_tile * s + base
            if it is None:
                if s >= 0:
                    eng.wait_ge(semaphore, n)
            else:
                assert n > 0
                wait_count(eng, semaphore, it * (per_tile * PERIOD) + n, alone)

        def wait_count(eng, semaphore, count, alone=False):
            if alone or eng is pool_engine:
                count = eng.to_reg(count)
                eng.wait_ge(routed, 1)
            eng.wait_ge(semaphore, count)

        def wait_dma(eng, semaphores, it, s):
            if it is None:
                if s >= 0:
                    eng.wait_ge(semaphores[s % PERIOD], 16 * (s // PERIOD) + 16)
            else:
                eng.wait_ge(semaphores[s % PERIOD], it * 16 + (16 * (s // PERIOD) + 16))

        def tile_at(it, s):
            return s if it is None else it * PERIOD + s

        def halves(bank2):
            return bank2[:, :, 0:HALF]

        def inside(it, s):
            return it is not None or 0 <= s < TILES

        pool_engine = nc.gpsimd
        block = ctx.enter_context(nc.Block())

        @block.tensor
        def _(pe):
            pe.wait_ge(consts, 1)
            pe.wait_ge(placed, 1)
            rank, totals = g_ps[:, 0, 0:TT * E], g_ps[:, 1, 0:TT * E]
            flat = onehot[:].rearrange("p j e -> p (j e)")
            pe.matmul(totals, ones[:], flat, start=True, stop=True)
            pe.matmul(rank, before[:], flat, start=True, stop=False, skip_group_check=True)
            for j in range(TT - 1):
                later = TT - 1 - j
                last = pe.matmul(rank[:, (j + 1) * E:].rearrange("p (j e) -> p j e", e=E), ones[:],
                                 onehot[:, j:j + 1, :].to_broadcast([P, later, E]), start=False,
                                 stop=(j == TT - 2), skip_group_check=True)
            last.then_inc(ranked, 1)
            pe.wait_ge(placed, 2)
            for j in range(TT):
                last = pe.matmul(u_ps[:, 0, 0:3 * TILES], place[:, j, :],
                                 marks[:, j].rearrange("p k s -> p (k s)"), start=(j == 0), stop=(j == TT - 1))
            last.then_inc(inverted, 1)
            pe.wait_ge(routed, 1)

            def expert(it, s):
                at = tile_at(it, s)
                column = tile_expert_i[0:1, at:at + 1] if it is None else tile_expert_i[0:1, bass.ds(at, 1)]
                return pe.value_load(column, min_val=0, max_val=E - 1)

            def part(s, it):
                if inside(it, s + 1):
                    wait_dma(pe, gathered, it, s + 1)
                    wait_n(pe, xT_ready, it, s)
                    for c in range(C):
                        last = pe.transpose(x_ps[:, c * P:(c + 1) * P], xg[:, (s + 1) % PERIOD, c * P:(c + 1) * P],
                                            ident[:])
                    last.then_inc(xT_psum, 1)
                if inside(it, s):
                    e = expert(it, s)
                    pe.wait_ge(experts_ready, e + 1)
                    wait_n(pe, xT_ready, it, s)
                    wait_n(pe, gate_act, it, s - 1)
                    for half in range(2):
                        for c in range(C):
                            last = pe.matmul(g_ps[:, half, 0:HALF], xT[:, s % 2, c, :],
                                             wg[:, bass.ds(e, 1), c, half * HALF:(half + 1) * HALF],
                                             start=(c == 0), stop=(c == C - 1))
                    last.then_inc(gate_ready, 1)
                if inside(it, s - 1):
                    wait_n(pe, h_ready, it, s - 1)
                    wait_n(pe, hT_low, it, s - 2)
                    wait_n(pe, hT_high, it, s - 2)
                    for k in range(HC):
                        n = P if k < HC - 1 else LAST
                        last = pe.transpose(t_ps[0:n, k // 4, (k % 4) * P:(k % 4 + 1) * P],
                                            h[:, (s - 1) % 2, k * P:k * P + n], ident[:])
                        if k == 3:
                            last.then_inc(hT_psum, 1)
                    last.then_inc(hT_psum, 1)
                if inside(it, s):
                    for half in range(2):
                        for c in range(C):
                            last = pe.matmul(u_ps[:, half, 0:HALF], xT[:, s % 2, c, :],
                                             wu[:, bass.ds(e, 1), c, half * HALF:(half + 1) * HALF],
                                             start=(c == 0), stop=(c == C - 1))
                    last.then_inc(up_ready, 1)
                if inside(it, s - 1):
                    e = expert(it, s - 1)
                    wait_n(pe, hT_low, it, s - 1)
                    wait_n(pe, hT_high, it, s - 1)
                    wait_n(pe, summed, it, s - 2)
                    for k in range(HC):
                        n = P if k < HC - 1 else LAST
                        last = pe.matmul(d_ps[:, 0:D], hT[0:n, (s - 1) % 2, k, :], wd[0:n, bass.ds(e, 1), k, :],
                                         start=(k == 0), stop=(k == HC - 1))
                    last.then_inc(down_ready, 1)

            run_slots(pe, part)

        @block.scalar
        def _(act):
            def part(s, it):
                if inside(it, s + 1):
                    wait_n(act, xT_psum, it, s + 1)
                    wait_n(act, up_ready, it, s - 1)
                    act.activation(xT[:, (s + 1) % 2].rearrange("p c t -> p (c t)"), x_ps[:, 0:C * P], ACT.Copy)\
                       .then_inc(xT_ready, 1)
                if inside(it, s):
                    wait_n(act, gate_ready, it, s)
                    wait_n(act, h_ready, it, s - 2)
                    act.activation(act_g[:, s % 2].rearrange("p (a n) -> p a n", a=2), halves(g_ps), ACT.Silu)\
                       .then_inc(gate_act, 1)
                if inside(it, s - 1):
                    wait_n(act, hT_psum, it, s - 1, 1, 2)
                    wait_n(act, down_ready, it, s - 3)
                    act.activation(hT[:, (s - 1) % 2, 0:4].rearrange("p k t -> p (k t)"), t_ps[:, 0, :], ACT.Copy)\
                       .then_inc(hT_low, 1)

            act.wait_ge(routed, 1)
            run_slots(act, part)

        @block.vector
        def _(dve):
            def one(n):
                dve.wait_ge(route_step, n)

            dve.wait_ge(consts, 3)
            dve.tensor_copy(iota_f[:], iota_i[:])
            dve.tensor_copy(row_f[:], row_i[:])
            dve.reduce_max(best[:], logits, axis=AX.X).then_inc(route_step, 1)
            one(1)
            per_expert = [P, TT, E]
            dve.tensor_tensor(pick[:], logits, best[:].unsqueeze(2).to_broadcast(per_expert), ALU.is_ge)\
               .then_inc(route_step, 1)
            one(2)
            dve.tensor_tensor(pick[:], pick[:], descend[:].unsqueeze(1).to_broadcast(per_expert), ALU.mult)\
               .then_inc(route_step, 1)
            one(3)
            dve.reduce_max(best[:], pick[:], axis=AX.X).then_inc(route_step, 1)
            one(4)
            dve.tensor_tensor(onehot[:], pick[:], best[:].unsqueeze(2).to_broadcast(per_expert), ALU.is_equal)\
               .then_inc(placed, 1)
            dve.wait_ge(ranked, 1)
            dve.reduce_sum(count[:], g_ps[:, 1, 0:TT * E].rearrange("p (j e) -> p e j", e=E), axis=AX.X)\
               .then_inc(route_step, 1)
            one(5)
            dve.tensor_scalar(count_i[:], count[:], float(P - 1), None, ALU.add).then_inc(route_step, 1)
            one(6)
            dve.tensor_scalar(count_i[:], count_i[:], SHIFT, None, ALU.arith_shift_right).then_inc(route_step, 1)
            one(7)
            dve.tensor_copy(ntiles[:], count_i[:]).then_inc(route_step, 1)
            one(8)
            dve.tensor_tensor(running[:], upto[:], ntiles[:].unsqueeze(1).to_broadcast([P, E, E]), ALU.mult)\
               .then_inc(route_step, 1)
            one(9)
            dve.reduce_sum(ends[:], running[:], axis=AX.X).then_inc(route_step, 1)
            one(10)
            dve.tensor_tensor(starts[:], ends[:], ntiles[:], ALU.subtract).then_inc(route_step, 1)
            one(11)
            dve.tensor_scalar(starts[:], starts[:], float(P), None, ALU.mult).then_inc(route_step, 1)
            one(12)
            dve.tensor_tensor(pick[:], g_ps[:, 0, 0:TT * E].rearrange("p (j e) -> p j e", e=E),
                              starts[:].unsqueeze(1).to_broadcast(per_expert), ALU.add).then_inc(route_step, 1)
            one(13)
            dve.tensor_tensor(pick[:], pick[:], onehot[:], ALU.mult).then_inc(route_step, 1)
            one(14)
            dve.reduce_sum(slot[:], pick[:], axis=AX.X).then_inc(route_step, 1)
            one(15)
            dve.tensor_copy(slot_i[:, 0, :], slot[:]).then_inc(route_step, 1)
            one(16)
            dve.tensor_scalar(slot_i[:, 1, :], slot_i[:, 0, :], SHIFT, None, ALU.arith_shift_right)
            dve.tensor_scalar(slot_i[:, 2, :], slot_i[:, 0, :], P - 1, None, ALU.bitwise_and).then_inc(route_step, 1)
            one(17)
            dve.tensor_copy(slot_f[:], slot_i[:, 1:3, :]).then_inc(route_step, 1)
            one(18)
            spread = [P, TT, TILES]
            dve.tensor_tensor(marks[:, :, 2, :], iota_f[:, 0:TILES].unsqueeze(1).to_broadcast(spread),
                              slot_f[:, 0, :].unsqueeze(2).to_broadcast(spread), ALU.is_equal)
            dve.tensor_tensor(place[:], iota_f[:].unsqueeze(1).to_broadcast([P, TT, P]),
                              slot_f[:, 1, :].unsqueeze(2).to_broadcast([P, TT, P]), ALU.is_equal)\
               .then_inc(route_step, 1)
            one(19)
            dve.tensor_tensor(marks[:, :, 0, :], marks[:, :, 2, :],
                              iota_f[:, 0:TT].unsqueeze(2).to_broadcast(spread), ALU.mult)
            dve.tensor_scalar(marks[:, :, 1, :], marks[:, :, 2, :], row_f[:], None, ALU.mult).then_inc(placed, 1)
            dve.tensor_tensor(behind[:], ends[:].unsqueeze(1).to_broadcast([P, TILES, E]),
                              iota_f[:, 0:TILES].unsqueeze(2).to_broadcast([P, TILES, E]), ALU.is_le)\
               .then_inc(route_step, 1)
            one(20)
            dve.reduce_sum(tile_expert[:], behind[:], axis=AX.X).then_inc(route_step, 1)
            one(21)
            dve.tensor_scalar(tile_expert_i[:], tile_expert[:], float(E - 1), None, ALU.min)
            dve.wait_ge(inverted, 1)
            dve.tensor_copy(found[:].rearrange("p k s -> p (k s)"), u_ps[:, 0, 0:3 * TILES]).then_inc(route_step, 1)
            one(22)
            dve.scalar_tensor_tensor(take_f[:, 0, :], found[:, 0, :], float(P), found[:, 1, :], ALU.mult, ALU.add)
            dve.tensor_scalar(take_f[:, 1, :], found[:, 2, :], -SKIP, SKIP, ALU.mult, ALU.add).then_inc(route_step, 1)
            one(23)
            dve.tensor_tensor(take_f[:, 1, :], take_f[:, 1, :], take_f[:, 0, :], ALU.add).then_inc(route_step, 1)
            one(24)
            dve.tensor_copy(take[:], take_f[:]).then_inc(routed, 1)

            def own(it, s, n, alone=False):
                wait_n(dve, norm_step, it, s, n, NORM, alone)

            def part(s, it):
                if inside(it, s - 1):
                    wait_n(dve, hT_psum, it, s - 1, 2, 2)
                    wait_n(dve, down_ready, it, s - 3)
                    high = hT[:, (s - 1) % 2, 4:HC - 1].rearrange("p k t -> p (k t)")
                    dve.tensor_copy(high, t_ps[:, 1, 0:(HC - 5) * P])
                    dve.tensor_copy(hT[0:LAST, (s - 1) % 2, HC - 1, :], t_ps[0:LAST, 1, (HC - 5) * P:(HC - 4) * P])\
                       .then_inc(hT_high, 1)
                if inside(it, s):
                    wait_n(dve, up_ready, it, s)
                    wait_n(dve, gate_act, it, s)
                    wait_n(dve, hT_psum, it, s - 2, 2, 2)
                    dve.tensor_tensor(h[:, s % 2].rearrange("p (a n) -> p a n", a=2), halves(u_ps),
                                      act_g[:, s % 2].rearrange("p (a n) -> p a n", a=2), ALU.mult)\
                       .then_inc(h_ready, 1)
                if inside(it, s - 1):
                    t = s - 1
                    out_y = y[:, t % PERIOD, :]
                    wait_n(dve, down_ready, it, t)
                    wait_dma(dve, scattered, it, t - PERIOD)
                    dve.tensor_tensor(out_y, d_ps[:, 0:D], xg[:, t % PERIOD, :], ALU.add).then_inc(summed, 1)
                    wait_n(dve, summed, it, t)
                    var, root, scratch = rs[:, 0:1], rs[:, 1:2], rs[:, 2:3]
                    dve.bn_stats(stats[:], out_y).then_inc(norm_step, 1)
                    own(it, t, 1, alone=True)
                    dve.bn_aggr(moments[:], stats[:]).then_inc(norm_step, 1)
                    own(it, t, 2)
                    dve.tensor_scalar(var, moments[:, 1:2], EPS, None, ALU.add).then_inc(norm_step, 1)
                    own(it, t, 3)
                    dve.tensor_scalar(scratch.bitcast(I32), var.bitcast(I32), 1, None, ALU.arith_shift_right)\
                       .then_inc(norm_step, 1)
                    own(it, t, 4)
                    dve.tensor_scalar(root.bitcast(I32), scratch.bitcast(I32), -1.0, float(0x5F3759DF),
                                      ALU.mult, ALU.add).then_inc(norm_step, 1)
                    for n in range(NEWTON):
                        own(it, t, 5 + 3 * n)
                        dve.tensor_tensor(scratch, root, root, ALU.mult).then_inc(norm_step, 1)
                        own(it, t, 6 + 3 * n)
                        dve.scalar_tensor_tensor(scratch, scratch, -0.5, var, ALU.mult, ALU.mult)\
                           .then_inc(norm_step, 1)
                        own(it, t, 7 + 3 * n)
                        dve.scalar_tensor_tensor(root, scratch, 1.5, root, ALU.add, ALU.mult)\
                           .then_inc(norm_step, 1)
                    own(it, t, NORM)
                    dve.tensor_scalar(out_y, out_y, moments[:, 0:1], root, ALU.subtract, ALU.mult)\
                       .then_inc(y_ready, 1)

            run_slots(dve, part)

        @block.gpsimd
        def _(pool):
            pool.memset(ident[:], 0.0)
            pool.memset(before[:], 1.0)
            pool.memset(ones[:], 1.0)
            pool.memset(upto[:], 1.0)
            pool.iota(iota_i[:], pattern=[[1, P]], base=0, channel_multiplier=0)
            for e in range(E):
                last = pool.memset(descend[:, e:e + 1], float(E - e))
            pool.iota(row_i[:], pattern=[[0, 1]], base=0, channel_multiplier=1).then_inc(consts, 1)
            pool.wait_ge(consts, 1)
            pool.affine_select(out=ident[:], in_=ident[:], compare_op=ALU.not_equal, fill=1.0, base=0,
                               pattern=[[-1, P]], channel_multiplier=1)
            pool.affine_select(out=before[:], in_=before[:], compare_op=ALU.is_ge, fill=0.0, base=-1,
                               pattern=[[1, P]], channel_multiplier=-1)
            pool.affine_select(out=upto[:], in_=upto[:], compare_op=ALU.is_ge, fill=0.0, base=0,
                               pattern=[[1, E], [-1, E]], channel_multiplier=0).then_inc(consts, 2)
            pool.wait_ge(routed, 1)

            def part(s, it):
                if inside(it, s + 3):
                    t = s + 3
                    wait_dma(pool, gathered, it, t - 2)
                    at = tile_at(it, t)
                    column = take[:, 0, at:at + 1] if it is None else take[:, 0, bass.ds(at, 1)]
                    pool.tensor_copy(now[:, 0, t % 2:t % 2 + 1], column).then_inc(index_copied, 1)
                    wait_index(it, s, 0)
                    wait_n(pool, summed, it, t - PERIOD)
                    pool.indirect_dma_start(out=xg[:, t % PERIOD, :], out_offset=None, in_=x2,
                                            in_offset=bass.IndirectOffsetOnAxis(ap=now[:, 0, t % 2:t % 2 + 1], axis=0),
                                            bounds_check=TOKENS - 1, oob_is_err=False)\
                        .then_inc(gathered[t % PERIOD], 16)
                if inside(it, s - 2):
                    t = s - 2
                    wait_dma(pool, scattered, it, t - 2)
                    at = tile_at(it, t)
                    column = take[:, 1, at:at + 1] if it is None else take[:, 1, bass.ds(at, 1)]
                    pool.tensor_copy(now[:, 1, t % 2:t % 2 + 1], column).then_inc(index_copied, 1)
                    wait_index(it, s, 1)
                    wait_n(pool, y_ready, it, t)
                    pool.indirect_dma_start(out=out,
                                            out_offset=bass.IndirectOffsetOnAxis(ap=now[:, 1, t % 2:t % 2 + 1], axis=0),
                                            in_=y[:, t % PERIOD, :], in_offset=None,
                                            bounds_check=TOKENS - 1, oob_is_err=False)\
                        .then_inc(scattered[t % PERIOD], 16)

            def wait_index(it, s, n):
                copies = min(s + 4, TILES) + max(0, s - 2) + n * (s >= 2)
                if it is None:
                    pool.wait_ge(index_copied, copies)
                else:
                    wait_count(pool, index_copied, it * (2 * PERIOD) + (s + 4 + s - 2 + n))

            run_slots(pool, part)
            for n in range(PERIOD):
                pool.wait_ge(scattered[n], 16 * len(range(n, TILES, PERIOD)))

        @block.sync
        def _(sp):
            for e in range(E):
                sp.dma_start(wg[:, e], gate_w[e].rearrange("(c p) i -> p c i", p=P)).then_inc(expert_loaded[e], 16)
                sp.dma_start(wu[:, e], up_w[e].rearrange("(c p) i -> p c i", p=P)).then_inc(expert_loaded[e], 16)
                sp.dma_start(wd[:, e, 0:HC - 1], down_w[e, 0:(HC - 1) * P, :].rearrange("(k p) d -> p k d", p=P))\
                  .then_inc(expert_loaded[e], 16)
                sp.dma_start(wd[0:LAST, e, HC - 1], down_w[e, (HC - 1) * P:HID, :]).then_inc(expert_loaded[e], 16)
            for e in range(E):
                sp.wait_ge(expert_loaded[e], 64)
                sp.sem_inc(experts_ready, 1)


def build(nc, a, out):
    x1 = nc.dram_tensor("x1_dram", [TOKENS, D], FP32, kind="Internal").ap()
    x2 = nc.dram_tensor("x2_dram", [TOKENS, D], FP32, kind="Internal").ap()
    with nc.sbuf_tensor("logits", [P, BATCH * T, EXPERTS], FP32) as logits:
        if STAGE == 1:
            attention_phase(nc, False, a["x"], a["xT"], a["wq"], a["wkv"], a["wo"], out)
            return
        attention_phase(nc, False, a["x"], a["xT"], a["wq"], a["wkv"], a["wo"], x1)
        attention_phase(nc, True, x1, a["ctxT"], a["xwq"], a["xwkv"], a["xwo"], out if STAGE == 2 else x2,
                        rope=a["rope"], mask=a["mask"], router=a["router"], logits=logits[:])
        if STAGE == 3:
            expert_phase(nc, x2, logits[:], a["gate_w"], a["up_w"], a["down_w"], out)


def rotary_tables():
    half = DH // 2
    exps = np.arange(1, DH + 1, 2, dtype=np.float32)[:half] / np.float32(DH)
    w = np.float32(1.0) / np.float32(10000.0) ** exps
    angles = np.arange(1, SEQ + 1, dtype=np.float32)[:, None] * w[None, :]
    cos = np.repeat(np.cos(angles), 2, axis=1)
    sin = np.stack([-np.sin(angles), np.sin(angles)], axis=-1).reshape(SEQ, DH)
    both = np.stack([cos, sin]).reshape(2, T, P, DH)
    return np.ascontiguousarray(both.transpose(2, 0, 1, 3)).astype(np.float32)


STAGE = 3


def kernel(**inputs):
    from concourse import bacc
    from concourse.bass_utils import run_bass_kernel_spmd

    def arr(name):
        return np.asarray(inputs[name])

    def transposed(a):
        return np.ascontiguousarray(a.T)

    x = arr("x").reshape(TOKENS, D)
    arrays = {
        "x": x,
        "xT": transposed(x),
        "wq": transposed(arr("L0_attn_wq")),
        "wkv": np.concatenate([arr("L0_attn_wk").T, arr("L0_attn_wv").T], axis=1),
        "wo": transposed(arr("L0_attn_wo")),
        "ctxT": transposed(arr("ctx_1024").reshape(TOKENS, D)),
        "xwq": arr("L0_xattn_W_q"),
        "xwkv": arr("L0_xattn_W_kv"),
        "xwo": arr("L0_xattn_W_c"),
        "mask": transposed(arr("mask_BxS2_bf1").reshape(BATCH * T, P)).view(np.uint8),
        "rope": rotary_tables(),
        "router": transposed(arr("L0_ffn_router_w")),
        "gate_w": arr("L0_ffn_gate_w").transpose(0, 2, 1),
        "up_w": arr("L0_ffn_up_w").transpose(0, 2, 1),
        "down_w": arr("L0_ffn_down_w").transpose(0, 2, 1),
    }
    arrays = {n: np.ascontiguousarray(v) for n, v in arrays.items()}
    nc = bacc.Bacc("TRN2", target_bir_lowering=False, num_devices=1, dynamic_dma_scratch_size=8192)
    a = {n: nc.dram_tensor(f"in_{n}", list(v.shape), mybir.dt.from_np(v.dtype), kind="ExternalInput").ap()
         for n, v in arrays.items()}
    out = nc.dram_tensor("out_dram", [TOKENS, D], FP32, kind="ExternalOutput").ap()
    build(nc, a, out)
    r = run_bass_kernel_spmd(nc, [{f"in_{n}": v for n, v in arrays.items()}], core_ids=[0])
    return r.results[0]["out_dram"].reshape(BATCH, SEQ, D)
```

```python
from contextlib import ExitStack

import numpy as np
import concourse.bass as bass
from concourse import mybir

FP32 = mybir.dt.float32
F32R = mybir.dt.float32r
BF16 = mybir.dt.bfloat16
I32 = mybir.dt.int32
U8 = mybir.dt.uint8
U32 = mybir.dt.uint32
ALU = mybir.AluOpType
ACT = mybir.ActivationFunctionType
AX = mybir.AxisListType

P = 128
BATCH, SEQ, D = 8, 512, 256
TOKENS = BATCH * SEQ
HEADS = 16
DH = D // HEADS
T = SEQ // P
C = D // P
GROUPS, GH = 4, 4
PAIRS = HEADS // 2
STACK = 64
MAX_ROW, MASK_ROW = 3 * DH, 3 * DH + 2
WINDOW = 64
SPAN = P + WINDOW
VCOLS = DH + 1
SCALE = float(DH) ** -0.5
EPS = 1e-5
EXPERTS = 8
MASKED = -1.0e30
RING_W, RING_P = 3, 8
BIAS_HI, BIAS_LO = float(0xEE600000), float(0x000B2800)


BUILD_STEPS = (2, 5)
NEWTON = 3
NORM_LAST = 6 + 3 * NEWTON

PLAN = (
    [
        [(1, "FK", 0, 4), (1, "FQ", 0, 4), (2, "SP", 1, 0), (2, "PV", -1, 2, 1), (2, "OE", -1, 2),
         (3, "SP", 1, 1), (4, "MN", 0, 0), (4, "FQ", 0, 5), (5, "TO", -1, 2), (5, "FK", 0, 5),
         (6, "PV", -1, 3, 0), (6, "MA", 0, 0), (7, "MD", 0, 0), (7, "HQ", 1, 0), (7, "PQ", 1, 0),
         (7, "HK", 1, 0), (7, "PK", 1, 0)],
        [(0, "HQ", 1, 1), (0, "PQ", 1, 1), (1, "FQ", 0, 6), (2, "OE", -1, 3), (2, "PV", -1, 3, 1),
         (2, "FK", 0, 6), (3, "FQ", 0, 7), (4, "MN", 0, 1), (4, "FK", 0, 7), (4, "HK", 1, 1), (4, "PK", 1, 1),
         (5, "MA", 0, 1), (5, "TO", -1, 3), (5, "HQ", 1, 2), (5, "PQ", 1, 2), (6, "MD", 0, 1),
         (6, "PV", 0, 0, 0), (6, "TP", -1, 0), (7, "TP", -1, 1)],
        [(0, "HK", 1, 2), (0, "PK", 1, 2), (1, "HQ", 1, 3), (1, "PV", 0, 0, 1), (2, "PQ", 1, 3),
         (2, "HO", -1, 0), (2, "OU", -1, 0), (3, "LN", -1, 0), (3, "HO", -1, 1), (3, "OU", -1, 1),
         (3, "HK", 1, 3), (3, "OE", 0, 0), (3, "LN", -1, 1), (3, "LN", -1, 2), (3, "PK", 1, 3),
         (4, "LN", -1, 3), (4, "MN", 0, 2), (4, "TO", 0, 0), (6, "MA", 0, 2), (6, "MD", 0, 2),
         (6, "PV", 0, 1, 0), (6, "LN", -1, 4), (7, "LN", -1, 5)],
        [(0, "LN", -1, 6), (0, "PV", 0, 1, 1), (0, "FK", 1, 0), (0, "LN", -1, 7), (1, "LN", -1, 8),
         (2, "LN", -1, 9), (2, "FQ", 1, 0), (2, "LN", -1, 10), (2, "OE", 0, 1), (3, "FQ", 1, 1),
         (3, "LN", -1, 11), (3, "LN", -1, 12), (3, "MN", 0, 3), (3, "LN", -1, 13), (4, "LN", -1, 14),
         (4, "TO", 0, 1), (4, "LN", -1, 15), (4, "FK", 1, 1), (5, "MA", 0, 3), (6, "MD", 0, 3), (6, "FQ", 1, 2),
         (6, "PV", 0, 2, 0), (7, "FK", 1, 2), (7, "FK", 1, 3), (7, "FQ", 1, 3)],
    ],
    [
        [(1, "FK", 0, 4), (1, "FQ", 0, 4), (2, "PV", -1, 2, 3), (2, "OE", -1, 2), (4, "FQ", 0, 5),
         (6, "PV", -1, 3, 0), (6, "SP", 1, 0), (6, "SP", 1, 1), (7, "FK", 0, 5), (9, "PV", -1, 3, 1),
         (10, "XT", 1, 0), (11, "XT", 1, 1), (12, "MN", 0, 0), (12, "TO", -1, 2), (14, "MA", 0, 0),
         (14, "MD", 0, 0), (14, "HQ", 1, 0), (14, "PQ", 1, 0), (15, "HK", 1, 0), (15, "PK", 1, 0),
         (15, "PV", -1, 3, 2)],
        [(1, "HQ", 1, 1), (1, "PQ", 1, 1), (2, "PV", -1, 3, 3), (2, "OE", -1, 3), (2, "FK", 0, 6),
         (4, "FQ", 0, 6), (5, "HK", 1, 1), (5, "PK", 1, 1), (6, "PV", 0, 0, 0), (8, "FQ", 0, 7),
         (9, "TO", -1, 3), (10, "FK", 0, 7), (11, "PV", 0, 0, 1), (12, "HQ", 1, 2), (12, "PQ", 1, 2),
         (13, "MN", 0, 1), (14, "PV", 0, 0, 2), (14, "MA", 0, 1), (14, "MD", 0, 1), (15, "HK", 1, 2),
         (15, "PK", 1, 2)],
        [(0, "TP", -1, 0), (1, "HQ", 1, 3), (1, "TP", -1, 1), (1, "PQ", 1, 3), (2, "OE", 0, 0),
         (2, "PV", 0, 0, 3), (2, "HO", -1, 0), (2, "OU", -1, 0), (4, "HO", -1, 1), (5, "HK", 1, 3),
         (5, "OU", -1, 1), (5, "PK", 1, 3), (6, "PV", 0, 1, 0), (6, "LN", -1, 0), (8, "TO", 0, 0),
         (9, "LN", -1, 1), (9, "PV", 0, 1, 1), (10, "LN", -1, 2), (11, "LN", -1, 3), (12, "MN", 0, 2),
         (12, "PV", 0, 1, 2), (13, "LN", -1, 4), (14, "MA", 0, 2), (14, "MD", 0, 2), (14, "LN", -1, 5)],
        [(0, "LN", -1, 6), (0, "PV", 0, 1, 3), (0, "LN", -1, 7), (0, "LN", -1, 8), (2, "OE", 0, 1),
         (3, "FQ", 1, 0), (3, "LN", -1, 9), (4, "FQ", 1, 1), (4, "FK", 1, 0), (5, "FK", 1, 1),
         (5, "LN", -1, 10), (5, "PV", 0, 2, 0), (6, "TO", 0, 1), (7, "LN", -1, 11), (7, "LN", -1, 12),
         (8, "LN", -1, 13), (9, "LN", -1, 14), (10, "PV", 0, 2, 1), (10, "LN", -1, 15), (11, "FQ", 1, 2),
         (12, "MN", 0, 3), (12, "FK", 1, 2), (13, "RX", -1, 0), (14, "FQ", 1, 3), (14, "PV", 0, 2, 2),
         (14, "MA", 0, 3), (14, "MD", 0, 3), (14, "RX", -1, 1), (15, "FK", 1, 3), (15, "LG", -1, 0)],
    ],
)


def slot_steps(b, g, cross):
    n = GH * (T if cross else T // 2)
    at = GROUPS * b + g
    last, coming = divmod(at - 1, GROUPS), divmod(at + 1, GROUPS)
    steps = [("LD", b + 1, 0), ("LR", b - 1, 0)] if g == 0 else []
    between = PLAN[cross][g]
    for i in range(n):
        steps.append(("S2", *last, i))
        steps.append(("S1", b, g, i + 4) if i + 4 < n else ("S1", *coming, i + 4 - n))
        steps += [(kind, b + back, *rest) for when, kind, back, *rest in between if when == i]
    return steps


def exists(s):
    return 0 <= s[1] < BATCH


FREES = dict(XT="dve", PQ="act", PK="act", FQ="act", FK="dve", MA="act", MD="dve", TO="dve", TP="dve",
             OU="dve", RX="act", LG="dve")
BOTH = ("XT", "TP")
HALF_OF = dict(HQ="PQ", HK="PK", HO="OU")


def events_of(s, cross):
    kind, rest = s[0], s[2:]
    if kind in FREES:
        yield "chunk_ready", rest
        if kind in BOTH:
            yield "act_took", rest
        yield FREES[kind] + "_took", rest
    if kind in ("PQ", "PK"):
        for n in range(BUILD_STEPS[cross] - 1):
            yield "pool_step", (*rest, n)
        yield "stack_built", rest
    elif kind == "SP":
        yield "dve_step", rest
        yield "split_done", rest
    elif kind == "TO":
        yield "dve_step", rest
    elif kind == "S1":
        yield "scores_ready", rest
        yield "max_taken", rest
    elif kind == "S2":
        yield "keyed_ready", rest
        yield "probs_ready", rest
    elif kind == "PV":
        yield "probs_used", rest
    elif kind == "OE":
        yield "sums_taken", rest
    elif kind == "MN":
        yield "dve_step", rest
        yield "max_placed", rest
    elif kind == "LN":
        if rest[0] < NORM_LAST:
            yield "dve_step", rest
        else:
            yield "normed", rest


def plan_counts(cross):
    order, banks, in_bank, holder = {}, {}, {}, {}
    steady = 3
    for b in range(-1, BATCH + 1):
        n = 0
        for g in range(GROUPS):
            for s in slot_steps(b, g, cross):
                if not exists(s):
                    n += s[0] in FREES
                    continue
                if s[1] == steady:
                    for label, key in events_of(s, cross):
                        order.setdefault((label, s[0]), []).append(key)
                if s[0] in FREES:
                    banks[s] = n % RING_W
                    in_bank[s] = holder.get(n % RING_W)
                    holder[n % RING_W] = s
                    n += 1
    return order, banks, in_bank


def attention_buffers(nc, ctx):
    shapes = dict(
        w_hi=([C, 4 * D], F32R), w_lo=([C, 4 * D], F32R),
        ident=([P], FP32), ident_r=([P], F32R),
        kv_raw=([C, SEQ], FP32),
        kv_hi=([C, SEQ], F32R), kv_lo=([C, SEQ], F32R),
        raw=([2, 2, D], FP32),
        qx=([2, T, HEADS * STACK], F32R),
        kx=([2, T, HEADS * STACK], F32R),
        qp=([HEADS, SEQ], F32R),
        kp=([PAIRS, SEQ], F32R),
        vx=([2, T, HEADS, VCOLS], FP32),
        probs=([RING_P, SEQ], FP32),
        row_max=([2, GH, T], FP32),
        sums=([SEQ], FP32),
        inv=([T, GH], FP32),
        att=([T, D], FP32),
        attT_hi=([C, SEQ], F32R), attT_lo=([C, SEQ], F32R),
        y=([T, D], FP32),
        stats=([T, 6], FP32), moments=([T, 2], FP32),
        rs=([3, T], FP32),
        x_in=([T, D], FP32), xT_hi=([C, SEQ], F32R), xT_lo=([C, SEQ], F32R),
        rot=([3, D], FP32),
        cos_m=([BATCH * T, DH], FP32),
        sin_m=([BATCH * T, DH], FP32),
        cos_sin=([2, T, DH], FP32),
        mask_u8=([BATCH * T], U8), valid=([BATCH * T], FP32), key_bias=([BATCH * T, 2], FP32),
        router_w=([C, 8], FP32), yT=([C, SEQ], FP32),
        ident_b=([P], BF16),
        band=([4, SPAN], BF16),
    )
    bufs = {label: ctx.enter_context(nc.sbuf_tensor(label, [P] + shape, dt))
            for label, (shape, dt) in shapes.items()}
    bufs["next_q"], bufs["next_kv"] = bufs["rot"][:, 0:C], bufs["yT"][:]
    bufs["next_o"] = bufs["cos_m"][:].rearrange("p (c a) d -> p c (a d)", c=C)
    bufs["loaded"] = [{label: ctx.enter_context(nc.semaphore(f"{phase}_{label}_loaded"))
                       for label in ("qkv", "o", "consts")} for phase in ("slide", "cross")]
    return bufs


def load_weights(sp, bufs, cross, wq, wkv, wo):
    loaded = bufs["loaded"][cross]
    sp.dma_start(bufs["next_q"], wq.rearrange("(c p) n -> p c n", p=P)).then_inc(loaded["qkv"], 16)
    sp.dma_start(bufs["next_kv"], wkv.rearrange("(c p) n -> p c n", p=P)).then_inc(loaded["qkv"], 16)
    sp.dma_start(bufs["next_o"], wo.rearrange("(c p) n -> p c n", p=P)).then_inc(loaded["o"], 16)


def attention_phase(nc, cross, bufs, x_rows, kvT, weights, out_rows, logits=None, after=None):
    name = "cross" if cross else "slide"
    wq, wkv, wo = weights
    items = T if cross else T // 2
    order, banks, in_bank = plan_counts(cross)
    rows = x_rows.rearrange("(b t p) d -> b p t d", t=T, p=P)
    rows_out = out_rows.rearrange("(b t p) d -> b p t d", t=T, p=P)
    kvT_v = kvT.rearrange("(c p) (b s) -> b p c s", p=P, s=SEQ)

    with ExitStack() as ctx:
        def sem(label):
            return ctx.enter_context(nc.semaphore(f"{name}_{label}"))

        w_hi, w_lo, ident, ident_r = bufs["w_hi"], bufs["w_lo"], bufs["ident"], bufs["ident_r"]
        kv_raw, kv_hi, kv_lo, raw, vx = bufs["kv_raw"], bufs["kv_hi"], bufs["kv_lo"], bufs["raw"], bufs["vx"]
        qx, kx, qp, kp = bufs["qx"], bufs["kx"], bufs["qp"], bufs["kp"]
        probs, row_max, sums, inv = bufs["probs"], bufs["row_max"], bufs["sums"], bufs["inv"]
        att, attT_hi, attT_lo, y = bufs["att"], bufs["attT_hi"], bufs["attT_lo"], bufs["y"]
        stats, moments, rs = bufs["stats"], bufs["moments"], bufs["rs"]
        if cross:
            x_in, xT_hi, xT_lo, rot = bufs["x_in"], bufs["xT_hi"], bufs["xT_lo"], bufs["rot"]
            cos_m, sin_m = bufs["cos_m"], bufs["sin_m"]
            cos_sin, mask_u8, valid, key_bias = bufs["cos_sin"], bufs["mask_u8"], bufs["valid"], bufs["key_bias"]
            router_w, yT = bufs["router_w"], bufs["yT"]
        else:
            xT_hi, xT_lo, ident_b, band = kv_hi, kv_lo, bufs["ident_b"], bufs["band"]

        s1 = ctx.enter_context(nc.psum_tensor(f"{name}_s1", [P, 2, SEQ], FP32))
        s2 = ctx.enter_context(nc.psum_tensor(f"{name}_s2", [P, 2, SEQ], FP32))
        po = ctx.enter_context(nc.psum_tensor(f"{name}_po", [P, SEQ], FP32))
        wk = ctx.enter_context(nc.psum_tensor(f"{name}_wk", [P, RING_W, SEQ], FP32))

        def by_kind(label):
            return {kind: sem(f"{label}_{kind}") for lab, kind in order if lab == label}

        chunk_ready, act_took, dve_took = by_kind("chunk_ready"), by_kind("act_took"), by_kind("dve_took")
        stack_built, split_done = by_kind("stack_built"), by_kind("split_done")
        scores_ready, max_taken = by_kind("scores_ready"), by_kind("max_taken")
        keyed_ready, probs_ready = by_kind("keyed_ready"), by_kind("probs_ready")
        probs_used, sums_taken = by_kind("probs_used"), by_kind("sums_taken")
        max_placed, normed = by_kind("max_placed"), by_kind("normed")
        dve_step, pool_step = by_kind("dve_step"), by_kind("pool_step")
        prep_step, prep_pool = sem("prep_step"), sem("prep_pool")
        kv_loaded, x_loaded, res_loaded, y_free = (
            sem("kv_loaded"), sem("x_loaded"), sem("res_loaded"), sem("y_free"))
        consts_made, w_split, padded = sem("consts_made"), sem("w_split"), sem("padded")
        w_high, band_edges = sem("w_high"), sem("band_edges")

        loaded = bufs["loaded"][cross]
        weight_parts = ((slice(0, D), bufs["next_q"], loaded["qkv"]),
                        (slice(D, 3 * D), bufs["next_kv"], loaded["qkv"]),
                        (slice(3 * D, 4 * D), bufs["next_o"], loaded["o"]))
        pool_engine, sync_engine = nc.gpsimd, nc.sync
        LOOP_FROM, LOOP_PERIOD = 1, 2

        def run_batches(eng, part):
            def batch(b, it):
                for g in range(GROUPS):
                    for s in slot_steps(b, g, cross):
                        if exists(s):
                            part(s, it)

            for b in range(-1, LOOP_FROM):
                batch(b, None)
            with eng.Fori(0, (BATCH - 2) // LOOP_PERIOD) as it:
                for b in range(LOOP_FROM, LOOP_FROM + LOOP_PERIOD):
                    batch(b, it)
            for b in (BATCH - 1, BATCH):
                batch(b, None)

        def wait_for(eng, semaphores, label, it, kind, b, *rest, alone=False):
            keys = order[label, kind]
            if (label, kind) == ("chunk_ready", "RX"):
                b += 1
            wait_times(eng, semaphores[kind], it, b, len(keys), keys.index(rest) + 1, alone)

        def wait_times(eng, semaphore, it, b, per_batch, base, alone=False):
            n = per_batch * b + base
            if it is None:
                if b >= 0:
                    eng.wait_ge(semaphore, n)
            else:
                assert n > 0
                count = it * (per_batch * LOOP_PERIOD) + n
                if alone or eng is pool_engine or eng is sync_engine:
                    count = eng.to_reg(count)
                    eng.wait_ge(consts_made, 1)
                eng.wait_ge(semaphore, count)

        def batch_at(it, b):
            return b if it is None else it * LOOP_PERIOD + b

        def by_head(stack):
            return stack.rearrange("p t (h r) -> p t h r", r=STACK)

        def ring_before(s, back):
            kind, b, g, i = s
            n = (GROUPS * b + g) * items * GH + i - back
            if n < 0:
                return None
            at, i = divmod(n, items * GH)
            return (kind, at // GROUPS, at % GROUPS, i)

        def by_dve(s):
            return s[0] == "PK" and s[1] == 0

        def build_stack(eng, s, it, rotated):
            kind, b, t = s
            is_key = kind == "PK"
            wait_for(eng, act_took, "act_took", it, *s)
            stack = by_head((kx if is_key else qx)[:, b % 2])
            at = batch_at(it, b) * T
            if t == 0:
                if is_key and cross:
                    eng.tensor_copy(stack[:, :, :, MASK_ROW:MASK_ROW + 2],
                                    key_bias[:, bass.ds(at, T), :].unsqueeze(2).to_broadcast([P, T, HEADS, 2]))
                if not is_key:
                    eng.memset(stack[:, :, :, MAX_ROW:MAX_ROW + 2].bitcast(FP32), 0.0)
                    if cross:
                        keep = valid[:, bass.ds(at, T)].unsqueeze(2).unsqueeze(3)
                        eng.tensor_copy(stack[:, :, :, MASK_ROW:MASK_ROW + 2],
                                        keep.to_broadcast([P, T, HEADS, 2]))
            source = raw[:, t % 2, int(is_key), :]
            heads = source.rearrange("p (h d) -> p h d", d=DH)
            a, z, low = (0, 2, 1) if is_key else (0, 1, 2)
            both = stack[:, t, :, 0:3 * DH].rearrange("p h (k d) -> p h k d", k=3)
            twice = both[:, :, a:z + 1:z - a, :]
            step = pool_step[kind]
            if cross:
                def table(m):
                    return m[:, bass.ds(at + t, 1), :].to_broadcast([P, HEADS, DH])

                def doubled(m):
                    return rotated[:, m, :].rearrange("p (h d) -> p h d", d=DH).unsqueeze(2).to_broadcast(
                        [P, HEADS, 2, DH])
                if b == 0 or t == 0:
                    tb, tt = divmod(T * b + t - 1, T)
                    wait_for(eng, stack_built, "stack_built", it, kind, tb, tt)
                if b > 0:
                    tb, tt = divmod(T * b + t - (0 if is_key else 1), T)
                    wait_for(eng, stack_built, "stack_built", it, "PQ" if is_key else "PK", tb, tt)
                pairs = source.rearrange("p (h i two) -> p h i two", h=HEADS, two=2)
                eng.tensor_tensor(rotated[:, 0, :].rearrange("p (h d) -> p h d", d=DH), heads, table(cos_m), ALU.mult)\
                   .then_inc(step, 1)
                eng.tensor_tensor(rotated[:, 1, :].rearrange("p (h i two) -> p h i two", h=HEADS, two=2),
                                  pairs[:, :, :, ::-1],
                                  table(sin_m).rearrange("p h (i two) -> p h i two", two=2), ALU.mult)\
                   .then_inc(step, 1)
                wait_for(eng, pool_step, "pool_step", it, *s, 1)
                eng.tensor_tensor(rotated[:, 2, :], rotated[:, 0, :], rotated[:, 1, :], ALU.add).then_inc(step, 1)
                eng.tensor_tensor(twice, doubled(0), doubled(1), ALU.add).then_inc(step, 1)
                wait_for(eng, pool_step, "pool_step", it, *s, 3)
                heads = rotated[:, 2, :].rearrange("p (h d) -> p h d", d=DH)
            else:
                eng.tensor_copy(twice, heads.unsqueeze(2).to_broadcast([P, HEADS, 2, DH])).then_inc(step, 1)
                wait_for(eng, pool_step, "pool_step", it, *s, 0)
            eng.tensor_tensor(both[:, :, low, :], heads, both[:, :, 0, :].bitcast(FP32), ALU.subtract)\
               .then_inc(stack_built[kind], 1)

        block = ctx.enter_context(nc.Block())

        @block.tensor
        def _(pe):
            def free_bank(s, it):
                held = in_bank[s]
                if held is not None:
                    if FREES[held[0]] == "act":
                        wait_for(pe, act_took, "act_took", it, *held)
                    else:
                        wait_for(pe, dve_took, "dve_took", it, *held)
                return wk[:, banks[s], :]

            def product3(out, a_hi, a_lo, w0, w1, t, chunks=range(C)):
                for c in chunks:
                    tok = slice(t * P, (t + 1) * P)
                    pe.matmul(out, a_hi[:, c, tok], w_hi[:, c, w0:w1], start=(c == 0), stop=False)
                    pe.matmul(out, a_hi[:, c, tok], w_lo[:, c, w0:w1], start=False, stop=False)
                    last = pe.matmul(out, a_lo[:, c, tok], w_hi[:, c, w0:w1], start=False, stop=(c == C - 1))
                return last

            def part(s, it):
                kind, b = s[0], s[1]
                halves = range(2)
                if kind in HALF_OF:
                    kind, i, halves = HALF_OF[kind], s[2], range(1)
                    bank = free_bank((kind, b, i), it)
                elif kind in FREES:
                    i = s[2]
                    if kind in HALF_OF.values():
                        bank, halves = wk[:, banks[s], :], range(1, 2)
                    else:
                        bank = free_bank(s, it)
                    bank_r = bank.bitcast(F32R)
                first = halves == range(1)
                if kind == "XT":
                    if i == 0:
                        wait_times(pe, x_loaded, it, b, 16, 16)
                    for t in range(T):
                        last = pe.transpose(bank[:, t * P:(t + 1) * P], x_in[:, t, i * P:(i + 1) * P], ident[:])
                elif kind == "PQ":
                    if i == 0 and first:
                        if cross:
                            wait_for(pe, dve_took, "dve_took", it, "XT", b, C - 1)
                        wait_for(pe, split_done, "split_done", it, "SP", b, C - 1)
                    last = product3(bank[:, 0:D], xT_hi, xT_lo, 0, D, i, halves)
                elif kind == "PK":
                    last = product3(bank[:, 0:2 * D], kv_hi, kv_lo, D, 3 * D, i, halves)
                elif kind in ("FQ", "FK", "MA", "MD"):
                    if kind in ("MA", "MD"):
                        wait_for(pe, max_placed, "max_placed", it, "MN", b, i)
                        i = 2 * i + int(kind == "MD")
                    else:
                        if s == ("FQ", 0, 0):
                            pe.wait_ge(padded, 2)
                            pe.wait_ge(consts_made, 1)
                        wait_for(pe, stack_built, "stack_built", it, "PQ" if kind == "FQ" else "PK", b, T - 1)
                    stacks = kx if kind == "FK" else qx
                    for t in range(T):
                        last = pe.transpose(bank_r[:, t * P:(t + 1) * P],
                                            stacks[:, b % 2, t, i * P:(i + 1) * P], ident_r[:])
                elif kind == "TO":
                    wait_for(pe, sums_taken, "sums_taken", it, "OE", b, i)
                    for t in range(T):
                        last = pe.transpose(bank[:, t * P:(t + 1) * P], sums[:, t * P:(t + 1) * P], ident[:])
                elif kind == "TP":
                    wait_for(pe, dve_took, "dve_took", it, "TO", b, GROUPS - 1)
                    for t in range(T):
                        last = pe.transpose(bank[:, t * P:(t + 1) * P], att[:, t, i * P:(i + 1) * P], ident[:])
                elif kind == "OU":
                    wait_for(pe, dve_took, "dve_took", it, "TP", b, C - 1)
                    if s == ("HO", 0, 0):
                        pe.wait_ge(w_split, 3)
                    for half in halves:
                        last = product3(bank[:, half * D:(half + 1) * D], attT_hi, attT_lo,
                                        3 * D, 4 * D, 2 * i + half)
                elif kind == "RX":
                    wait_for(pe, normed, "normed", it, "LN", b, NORM_LAST)
                    for t in range(T):
                        last = pe.transpose(bank[:, t * P:(t + 1) * P], y[:, t, i * P:(i + 1) * P], ident[:])
                elif kind == "LG":
                    wait_for(pe, act_took, "act_took", it, "RX", b, C - 1)
                    for t in range(T):
                        for c in range(C):
                            last = pe.matmul(bank[:, 8 * t:8 * t + 8], yT[:, c, t * P:(t + 1) * P],
                                             router_w[:, c, :], start=(c == 0), stop=(c == C - 1))
                elif kind == "S1":
                    g, i = s[2], s[3]
                    c, j = divmod(i, items)
                    h = GH * g + c
                    if j == 0:
                        wait_for(pe, act_took, "act_took", it, "FQ", b, h // 2)
                        wait_for(pe, dve_took, "dve_took", it, "FK", b, h // 2)
                    before = ring_before(s, 2)
                    if before:
                        wait_for(pe, max_taken, "max_taken", it, *before)
                    out = s1[:, i % 2, :]
                    if cross:
                        last = pe.matmul(out, qp[:, h, j * P:(j + 1) * P], kp[:, h // 2, :],
                                         start=True, stop=True)
                    else:
                        for half in range(2):
                            t = 2 * j + half
                            at, keys = 2 * P * half, max(0, (t - 1) * P)
                            last = pe.matmul(out[:, at:at + 2 * P], qp[:, h, t * P:(t + 1) * P],
                                             kp[:, h // 2, keys:keys + 2 * P], start=True, stop=True)
                    last.then_inc(scores_ready[kind], 1)
                    return
                elif kind == "S2":
                    g, i = s[2], s[3]
                    j, c = divmod(i, GH)
                    h = GH * g + c
                    if s == ("S2", 0, 0, 0) and not cross:
                        pe.wait_ge(band_edges, 2)
                    if i == 0:
                        wait_for(pe, act_took, "act_took", it, "MA", b, g)
                    if i == 2:
                        wait_for(pe, dve_took, "dve_took", it, "MD", b, g)
                    before = ring_before(s, 2)
                    if before:
                        wait_for(pe, probs_ready, "probs_ready", it, *before)
                    out = s2[:, i % 2, :]
                    if cross:
                        last = pe.matmul(out, kp[:, h // 2, j * P:(j + 1) * P], qp[:, h, :],
                                         start=True, stop=True)
                    else:
                        for half in range(2):
                            t = 2 * j + half
                            at = 3 * WINDOW if t == 3 else 2 * P * half
                            queries = min(t * P, SEQ - 2 * P)
                            seen = at + (WINDOW if t == T - 1 else 0)
                            pe.matmul(out[:, at:at + 2 * P], kp[:, h // 2, t * P:(t + 1) * P],
                                      qp[:, h, queries:queries + 2 * P], start=True, stop=False)
                            last = pe.matmul(out[:, seen:seen + SPAN], ident_b[:],
                                             band[:, 3 if t == T - 1 else 2, :], start=False, stop=True)
                    last.then_inc(keyed_ready[kind], 1)
                    return
                elif kind == "PV":
                    g, j = s[2], s[3]
                    wait_for(pe, probs_ready, "probs_ready", it, "S2", b, g, GH * j + GH - 1)
                    if j == 0:
                        wait_for(pe, act_took, "act_took", it, "PK", b, T - 1)
                        gb, gg = divmod(4 * b + g - 1, GROUPS)
                        wait_for(pe, sums_taken, "sums_taken", it, "OE", gb, gg)
                    for half in range(1 if cross else 2):
                        t = j if cross else 2 * j + half
                        for c in range(GH):
                            slot = (items * GH * g + GH * j + c) % RING_P
                            if cross:
                                out, p = po[32 * c:32 * c + VCOLS, :], probs[:, slot, :]
                            else:
                                q0 = min(t * P, SEQ - SPAN)
                                out = po[32 * c:32 * c + VCOLS, q0:q0 + SPAN]
                                p = probs[:, slot, half * SPAN:(half + 1) * SPAN]
                            last = pe.matmul(out, vx[:, b % 2, t, GH * g + c, :], p, start=(t == 0),
                                             stop=(t == T - 1), tile_position=(0, 32 * c),
                                             skip_group_check=True)
                    last.then_inc(probs_used[kind], 1)
                    return
                else:
                    return
                if not first:
                    last.then_inc(chunk_ready[kind], 1)

            pe.wait_ge(w_split, 2)
            run_batches(pe, part)

        @block.scalar
        def _(act):
            def part(s, it):
                kind, b = s[0], s[1]
                if kind in FREES:
                    i = s[2]
                    bank = wk[:, banks[s], :]
                    if kind in BOTH or FREES[kind] == "act":
                        wait_for(act, chunk_ready, "chunk_ready", it, *s)
                if kind == "XT":
                    act.activation(xT_hi[:, i, :], bank, ACT.Copy).then_inc(act_took[kind], 1)
                elif kind == "PQ" or kind == "PK":
                    tb, tt = divmod(T * b + i - 2, T)
                    wait_for(act, stack_built, "stack_built", it, kind, tb, tt)
                    if kind == "PK":
                        act.activation(vx[:, b % 2, i, :, 0:DH],
                                       bank[:, D:2 * D].rearrange("p (h d) -> p h d", d=DH), ACT.Copy)
                    act.activation(raw[:, i % 2, int(kind == "PK"), :], bank[:, 0:D], ACT.Copy)\
                       .then_inc(act_took[kind], 1)
                elif kind == "FQ" or kind == "MA":
                    r = 0
                    if kind == "MA":
                        r, i = 32, 2 * i
                    act.activation(qp[r:64, 2 * i, :], bank[r:64, :], ACT.Copy)
                    act.activation(qp[64 + r:P, 2 * i + 1, :], bank[64 + r:P, :], ACT.Copy)\
                       .then_inc(act_took[kind], 1)
                elif kind == "TP":
                    act.activation(attT_hi[:, i, :], bank, ACT.Copy).then_inc(act_took[kind], 1)
                elif kind == "RX":
                    act.activation(yT[:, i, :], bank, ACT.Copy).then_inc(act_took[kind], 1)
                elif kind == "S2":
                    wait_for(act, keyed_ready, "keyed_ready", it, *s)
                    g, i = s[2], s[3]
                    before = ring_before(s, RING_P)
                    if before:
                        wait_for(act, probs_used, "probs_used", it, "PV", before[1], before[2], before[3] // GH)
                    slot = (items * GH * g + i) % RING_P
                    if cross:
                        out, in_ = probs[:, slot, :], s2[:, i % 2, :]
                    else:
                        out = probs[:, slot, 0:2 * SPAN].rearrange("p (a n) -> p a n", a=2)
                        in_ = s2[:, i % 2, :].rearrange("p (a n) -> p a n", a=2)[:, :, 0:SPAN]
                    act.activation(out, in_, ACT.Exp, scale=SCALE).then_inc(probs_ready[kind], 1)
                elif kind == "OE":
                    g = s[2]
                    wait_for(act, probs_used, "probs_used", it, "PV", b, g, items - 1)
                    gb, gg = divmod(GROUPS * b + g - 1, GROUPS)
                    wait_for(act, chunk_ready, "chunk_ready", it, "TO", gb, gg)
                    act.activation(sums[:], po[:], ACT.Copy).then_inc(sums_taken[kind], 1)

            for n, (columns, stage, weights_loaded) in enumerate(weight_parts):
                act.wait_ge(weights_loaded, 16 if n == 2 else 32)
                act.activation(w_hi[:, :, columns], stage, ACT.Copy).then_inc(w_high, 1)
            run_batches(act, part)

        @block.vector
        def _(dve):
            dve.memset(po[:], 0.0)
            if cross:
                dve.sem_inc(padded, 2)
            for n, (columns, stage, _) in enumerate(weight_parts):
                dve.wait_ge(w_high, n + 1)
                dve.tensor_tensor(w_lo[:, :, columns], stage, w_hi[:, :, columns].bitcast(FP32),
                                  ALU.subtract).then_inc(w_split, 1)
            dve.wait_ge(w_split, 3)
            if cross:
                dve.wait_ge(loaded["consts"], 48)
                dve.tensor_copy(valid[:], mask_u8[:]).then_inc(prep_step, 1)
                dve.wait_ge(prep_step, 1)
                for part_, bias in enumerate((BIAS_HI, BIAS_LO)):
                    dve.tensor_scalar(key_bias[:, :, part_:part_ + 1], valid[:].unsqueeze(2), bias, -bias,
                                      ALU.mult, ALU.add)
                for k, table in enumerate((cos_m, sin_m)):
                    for b in range(BATCH):
                        keep = valid[:, T * b:T * b + T].unsqueeze(2).to_broadcast([P, T, DH])
                        last = dve.tensor_tensor(table[:, T * b:T * b + T, :], cos_sin[:, k, :, :], keep, ALU.mult)
                last.then_inc(consts_made, 1)
            else:
                dve.wait_ge(prep_pool, 2)
                dve.tensor_copy(ident_b[:], ident[:])
                dve.tensor_copy(ident_r[:], ident[:]).then_inc(consts_made, 1)

            def part(s, it):
                kind, b = s[0], s[1]
                if kind in FREES:
                    i = s[2]
                    bank = wk[:, banks[s], :]
                    if kind in BOTH:
                        wait_for(dve, act_took, "act_took", it, *s)
                    elif FREES[kind] == "dve":
                        wait_for(dve, chunk_ready, "chunk_ready", it, *s)
                if kind == "PK" and by_dve(s):
                    build_stack(dve, s, it, att)
                elif kind == "XT":
                    dve.tensor_tensor(xT_lo[:, i, :], bank, xT_hi[:, i, :].bitcast(FP32), ALU.subtract)\
                       .then_inc(dve_took[kind], 1)
                elif kind == "SP":
                    i = s[2]
                    wait_times(dve, kv_loaded, it, b, 16, 16)
                    wait_for(dve, chunk_ready, "chunk_ready", it, "PK", b - 1, T - 1)
                    dve.tensor_copy(kv_hi[:, i], kv_raw[:, i]).then_inc(dve_step[kind], 1)
                    wait_for(dve, dve_step, "dve_step", it, *s)
                    dve.tensor_tensor(kv_lo[:, i], kv_raw[:, i], kv_hi[:, i].bitcast(FP32), ALU.subtract)\
                       .then_inc(split_done[kind], 1)
                    if s == ("SP", 0, C - 1) and not cross:
                        rows_ = qp[STACK:P].rearrange("p (i two) n -> p i two n", two=2)[:, :, 0, :]
                        dve.memset(rows_.bitcast(FP32), 0.0).then_inc(padded, 1)
                elif kind == "MD":
                    j = 2 * i + 1
                    dve.tensor_copy(qp[32:64, 2 * j, :], bank[32:64, :])
                    dve.tensor_copy(qp[96:P, 2 * j + 1, :], bank[96:P, :]).then_inc(dve_took[kind], 1)
                elif kind == "FK":
                    dve.tensor_copy(kp[:, i, :], bank).then_inc(dve_took[kind], 1)
                elif kind == "TO":
                    v = bank.rearrange("p (t c r) -> p t c r", t=T, c=GH)
                    gb, gg = divmod(GROUPS * b + i - 1, GROUPS)
                    wait_for(dve, dve_took, "dve_took", it, "TO", gb, gg)
                    dve.reciprocal(inv[:].unsqueeze(3), v[:, :, :, DH:DH + 1]).then_inc(dve_step[kind], 1)
                    wait_for(dve, dve_step, "dve_step", it, *s)
                    out = att[:, :, DH * GH * i:DH * GH * (i + 1)].rearrange("p t (c d) -> p t c d", c=GH)
                    dve.tensor_tensor(out, v[:, :, :, 0:DH], inv[:].unsqueeze(3).to_broadcast([P, T, GH, DH]),
                                      ALU.mult).then_inc(dve_took[kind], 1)
                elif kind == "TP":
                    dve.tensor_tensor(attT_lo[:, i, :], bank, attT_hi[:, i, :].bitcast(FP32), ALU.subtract)\
                       .then_inc(dve_took[kind], 1)
                elif kind == "OU":
                    if i == 0:
                        wait_times(dve, res_loaded, it, b, 16, 16)
                    out = y[:, 2 * i:2 * i + 2, :]
                    dve.tensor_tensor(out, bank.rearrange("p (t d) -> p t d", t=2), out, ALU.add)\
                       .then_inc(dve_took[kind], 1)
                elif kind == "LG":
                    dve.tensor_copy(logits[:, bass.ds(batch_at(it, b) * T, T), :],
                                    bank[:, 0:8 * T].rearrange("p (t e) -> p t e", e=8)).then_inc(dve_took[kind], 1)
                elif kind == "S1":
                    g, i = s[2], s[3]
                    c, j = divmod(i, items)
                    if s == ("S1", 0, 0, 0) and not cross:
                        dve.wait_ge(band_edges, 2)
                    wait_for(dve, scores_ready, "scores_ready", it, *s, alone=not cross)
                    if cross:
                        dve.reduce_max(row_max[:, g % 2, c, j:j + 1], s1[:, i % 2, :], axis=AX.X)\
                           .then_inc(max_taken[kind], 1)
                    else:
                        for half in range(2):
                            t = 2 * j + half
                            at = 2 * P * half + (0 if t == 0 else WINDOW)
                            seen = s1[:, i % 2, at:at + SPAN]
                            last = dve.tensor_tensor_reduce(
                                out=seen, in0=seen, in1=band[:, 1 if t == 0 else 0, :], scale=1.0, scalar=MASKED,
                                op0=ALU.add, op1=ALU.max, accum_out=row_max[:, g % 2, c, t:t + 1])
                        last.then_inc(max_taken[kind], 1)
                elif kind == "MN":
                    g = s[2]
                    wait_for(dve, max_taken, "max_taken", it, "S1", b, g, items * GH - 1)
                    rows_ = by_head(qx[:, b % 2])[:, :, GH * g:GH * g + GH, MAX_ROW:MAX_ROW + 2]
                    m = row_max[:, g % 2].rearrange("p c t -> p t c").unsqueeze(3)
                    dve.tensor_scalar(rows_[:, :, :, 0:1], m, -1.0, None, ALU.mult).then_inc(dve_step[kind], 1)
                    wait_for(dve, dve_step, "dve_step", it, *s)
                    dve.scalar_tensor_tensor(rows_[:, :, :, 1:2], m, -1.0, rows_[:, :, :, 0:1].bitcast(FP32),
                                             ALU.mult, ALU.subtract).then_inc(max_placed[kind], 1)
                elif kind == "LN":
                    k = s[2]
                    var, root, scratch = rs[:, 0, :], rs[:, 1, :], rs[:, 2, :]
                    if k < 2:
                        wait_for(dve, dve_took, "dve_took", it, "OU", b, k)
                        for t in (2 * k, 2 * k + 1):
                            last = dve.bn_stats(stats[:, t, :], y[:, t, :])
                        last.then_inc(dve_step[kind], 1)
                        return
                    wait_for(dve, dve_step, "dve_step", it, "LN", b, k - 1, alone=(k == 2))
                    if k == 2:
                        for t in range(T):
                            last = dve.bn_aggr(moments[:, t, :], stats[:, t, :])
                        last.then_inc(dve_step[kind], 1)
                    elif k == 3:
                        dve.tensor_scalar(var.unsqueeze(2), moments[:, :, 1:2], EPS, None, ALU.add)\
                           .then_inc(dve_step[kind], 1)
                    elif k == 4:
                        dve.tensor_scalar(scratch.bitcast(I32), var.bitcast(I32), 1, None, ALU.arith_shift_right)\
                           .then_inc(dve_step[kind], 1)
                    elif k == 5:
                        dve.tensor_scalar(root.bitcast(I32), scratch.bitcast(I32), -1.0, float(0x5F3759DF),
                                          ALU.mult, ALU.add).then_inc(dve_step[kind], 1)
                    elif k == NORM_LAST:
                        for t in range(T):
                            last = dve.tensor_scalar(y[:, t, :], y[:, t, :], moments[:, t, 0:1], rs[:, 1, t:t + 1],
                                                     ALU.subtract, ALU.mult)
                        last.then_inc(normed[kind], 1)
                    elif k % 3 == 0:
                        dve.tensor_tensor(scratch, root, root, ALU.mult).then_inc(dve_step[kind], 1)
                    elif k % 3 == 1:
                        dve.scalar_tensor_tensor(scratch, scratch, -0.5, var, ALU.mult, ALU.mult)\
                           .then_inc(dve_step[kind], 1)
                    else:
                        dve.scalar_tensor_tensor(root, scratch, 1.5, root, ALU.add, ALU.mult)\
                           .then_inc(dve_step[kind], 1)

            run_batches(dve, part)

        @block.gpsimd
        def _(pool):
            if cross:
                pool.wait_ge(consts_made, 1)
            else:
                pool.memset(ident[:], 0.0)
                pool.memset(band[:], 0.0).then_inc(prep_pool, 1)
                pool.wait_ge(prep_pool, 1)
                pool.affine_select(out=ident[:], in_=ident[:], compare_op=ALU.not_equal, fill=1.0, base=0,
                                   pattern=[[-1, P]], channel_multiplier=1).then_inc(prep_pool, 1)
                for half in range(2):
                    for stack in (qx, kx):
                        pads = by_head(stack[:, half])
                        pool.memset(pads[:, :, :, MAX_ROW + 2:STACK].bitcast(FP32), 0.0)
                    pool.memset(pads[:, :, :, MAX_ROW:MAX_ROW + 2].bitcast(FP32), 1.0)
                    pool.memset(vx[:, half, :, :, DH:VCOLS], 1.0)
                edges = ((-1, -1, 1), (0, 1, -1), (0, -1, 1), (-WINDOW, -1, 1))
                others = ((WINDOW, 1, -1), (WINDOW - 1, -1, 1), (WINDOW - 1, 1, -1), (P - 1, 1, -1))
                for step, bounds in enumerate((edges, others)):
                    if step:
                        pool.wait_ge(band_edges, 1)
                    for n, (base, row, col) in enumerate(bounds):
                        last = pool.affine_select(out=band[:, n, :], in_=band[:, n, :], compare_op=ALU.is_ge,
                                                  fill=MASKED, base=base, pattern=[[col, SPAN]], channel_multiplier=row)
                    last.then_inc(band_edges, 1)
                pool.memset(qp[0:STACK].rearrange("p (i two) n -> p i two n", two=2)[:, :, 1, :].bitcast(FP32), 0.0)\
                    .then_inc(padded, 1)

            def part(s, it):
                if s[0] in ("PQ", "PK") and not by_dve(s):
                    build_stack(pool, s, it, rot if cross else None)

            run_batches(pool, part)

        @block.sync
        def _(sp):
            sp.sem_inc(y_free, 16)
            if cross:
                sp.sem_inc(chunk_ready["RX"], C)
            if not cross:
                load_weights(sp, bufs, False, wq, wkv, wo)

            def part(s, it):
                kind, b = s[0], s[1]
                if kind == "LD":
                    wait_for(sp, split_done, "split_done", it, "SP", b - 1, C - 1)
                    sp.dma_start(kv_raw[:], at_batch(kvT_v, it, b)).then_inc(kv_loaded, 16)
                    if s == ("LD", 1, 0) and after:
                        load_next()
                    if cross:
                        wait_for(sp, chunk_ready, "chunk_ready", it, "XT", b - 1, C - 1)
                        sp.dma_start(x_in[:], at_batch(rows, it, b)).then_inc(x_loaded, 16)
                elif kind == "LR":
                    wait_times(sp, y_free, it, b, 16, 16)
                    if cross:
                        wait_for(sp, chunk_ready, "chunk_ready", it, "RX", b - 1, C - 1)
                    sp.dma_start(y[:], at_batch(rows, it, b)).then_inc(res_loaded, 16)
                elif kind == "LN" and s[2] == NORM_LAST:
                    wait_for(sp, normed, "normed", it, *s)
                    sp.dma_start(at_batch(rows_out, it, b), y[:]).then_inc(y_free, 16)

            def at_batch(view, it, b):
                return view[b] if it is None else view[bass.ds(it * LOOP_PERIOD + b, 1)].squeeze(0)

            def load_next():
                sp.wait_ge(w_split, 3)
                load_weights(sp, bufs, True, *after[0:3])
                for buffer, source in ((bufs["mask_u8"], after[3]), (bufs["cos_sin"], after[4]),
                                       (bufs["router_w"], after[5].rearrange("(c p) e -> p c e", p=P))):
                    sp.dma_start(buffer[:], source).then_inc(bufs["loaded"][True]["consts"], 16)

            run_batches(sp, part)
            sp.wait_ge(y_free, 16 * (BATCH + 1))


def expert_phase(nc, x2, logits, gate_w, up_w, down_w, out):
    E, HID = EXPERTS, gate_w.shape[2]
    TT = BATCH * T
    TILES = TT + E - 1
    HALF = HID // 2
    HC = -(-HID // P)
    LAST = HID - (HC - 1) * P
    SHIFT = P.bit_length() - 1
    SKIP = 2.0 * TOKENS
    PERIOD = 4
    NORM = 2 + 3 + 3 * NEWTON

    with ExitStack() as ctx:
        def sb(label, shape, dt):
            return ctx.enter_context(nc.sbuf_tensor(f"moe_{label}", shape, dt))

        def sem(label):
            return ctx.enter_context(nc.semaphore(f"moe_{label}"))

        def pb(label, shape):
            return ctx.enter_context(nc.psum_tensor(f"moe_{label}", shape, FP32))

        wg = sb("wg", [P, E, C, HID], FP32)
        wu = sb("wu", [P, E, C, HID], FP32)
        wd = sb("wd", [P, E, HC, D], FP32)
        ident = sb("ident", [P, P], FP32)
        best = sb("best", [P, TT], FP32)
        pick = sb("pick", [P, TT, E], FP32)
        onehot = sb("onehot", [P, TT, E], BF16)
        before = sb("before", [P, P], BF16)
        ones = sb("ones", [P, P], BF16)
        descend = sb("descend", [P, E], FP32)
        upto = sb("upto", [P, E, E], FP32)
        count = sb("count", [P, E], FP32)
        count_i = sb("count_i", [P, E], I32)
        ntiles = sb("ntiles", [P, E], FP32)
        running = sb("running", [P, E, E], FP32)
        ends = sb("ends", [P, E], FP32)
        starts = sb("starts", [P, E], FP32)
        slot = sb("slot", [P, TT], FP32)
        slot_i = sb("slot_i", [P, 3, TT], I32)
        slot_b = sb("slot_b", [P, 2, TT], BF16)
        iota_i = sb("iota_i", [P, P], I32)
        iota_f = sb("iota_f", [P, P], FP32)
        iota_b = sb("iota_b", [P, P], BF16)
        row_i = sb("row_i", [P, 1], I32)
        row_f = sb("row_f", [P, 1], FP32)
        behind = sb("behind", [P, TILES, E], FP32)
        tile_expert = sb("tile_expert", [P, TILES], FP32)
        tile_expert_i = sb("tile_expert_i", [P, TILES], I32)
        place = sb("place", [P, TT, P], BF16)
        marks = sb("marks", [P, TT, 3, TILES], BF16)
        found = sb("found", [P, 3, TILES], FP32)
        take_f = sb("take_f", [P, 2, TILES], FP32)
        take = sb("take", [P, 2, TILES], U32)
        now = sb("now", [P, 2, 2], U32)
        xg = sb("xg", [P, PERIOD, D], FP32)
        xT = sb("xT", [P, 2, C, P], FP32)
        act_g = sb("act_g", [P, 2, HID], FP32)
        h = sb("h", [P, 2, HID], FP32)
        hT = sb("hT", [P, 2, HC, P], FP32)
        y = sb("y", [P, PERIOD, D], FP32)
        stats = sb("stats", [P, 6], FP32)
        moments = sb("moments", [P, 2], FP32)
        rs = sb("rs", [P, 3], FP32)

        g_ps, u_ps, t_ps = pb("g", [P, 2, SEQ]), pb("u", [P, 2, SEQ]), pb("t", [P, 2, SEQ])
        x_ps, d_ps = pb("x", [P, SEQ]), pb("d", [P, SEQ])

        consts, route_step, ranked = sem("consts"), sem("route_step"), sem("ranked")
        placed = sem("placed")
        inverted, routed = sem("inverted"), sem("routed")
        expert_loaded = [sem(f"expert_loaded{e}") for e in range(E)]
        experts_ready = sem("experts_ready")
        gathered = [sem(f"gathered{n}") for n in range(PERIOD)]
        scattered = [sem(f"scattered{n}") for n in range(PERIOD)]
        index_copied, xT_psum, xT_ready = sem("index_copied"), sem("xT_psum"), sem("xT_ready")
        gate_ready, up_ready, gate_act = sem("gate_ready"), sem("up_ready"), sem("gate_act")
        h_ready, hT_psum, hT_low, hT_high = sem("h_ready"), sem("hT_psum"), sem("hT_low"), sem("hT_high")
        down_ready, summed, norm_step, y_ready = sem("down_ready"), sem("summed"), sem("norm_step"), sem("y_ready")

        def run_slots(eng, part):
            first = PERIOD + 1
            turns = (TILES - 3 - first) // PERIOD
            behind_loop = first + turns * PERIOD
            for s in range(-3, first):
                part(s, None)
            with eng.Fori(0, turns) as it:
                for s in range(first, first + PERIOD):
                    part(s, it)
            for s in range(behind_loop, TILES + 2):
                part(s, None)

        def wait_n(eng, semaphore, it, s, base=1, per_tile=1, alone=False):
            n = per_tile * s + base
            if it is None:
                if s >= 0:
                    eng.wait_ge(semaphore, n)
            else:
                assert n > 0
                wait_count(eng, semaphore, it * (per_tile * PERIOD) + n, alone)

        def wait_count(eng, semaphore, count, alone=False):
            if alone or eng is pool_engine:
                count = eng.to_reg(count)
                eng.wait_ge(routed, 1)
            eng.wait_ge(semaphore, count)

        def wait_dma(eng, semaphores, it, s):
            if it is None:
                if s >= 0:
                    eng.wait_ge(semaphores[s % PERIOD], 16 * (s // PERIOD) + 16)
            else:
                eng.wait_ge(semaphores[s % PERIOD], it * 16 + (16 * (s // PERIOD) + 16))

        def tile_at(it, s):
            return s if it is None else it * PERIOD + s

        def halves(bank2):
            return bank2[:, :, 0:HALF]

        def inside(it, s):
            return it is not None or 0 <= s < TILES

        pool_engine = nc.gpsimd
        block = ctx.enter_context(nc.Block())

        @block.tensor
        def _(pe):
            pe.wait_ge(consts, 1)
            pe.wait_ge(placed, 1)
            rank, totals = g_ps[:, 0, 0:TT * E], g_ps[:, 1, 0:TT * E]
            flat = onehot[:].rearrange("p j e -> p (j e)")
            pe.matmul(totals, ones[:], flat, start=True, stop=True)
            pe.matmul(rank, before[:], flat, start=True, stop=False, skip_group_check=True)
            for j in range(TT - 1):
                later = TT - 1 - j
                last = pe.matmul(rank[:, (j + 1) * E:].rearrange("p (j e) -> p j e", e=E), ones[:],
                                 onehot[:, j:j + 1, :].to_broadcast([P, later, E]), start=False,
                                 stop=(j == TT - 2), skip_group_check=True)
            last.then_inc(ranked, 1)
            pe.wait_ge(placed, 2)
            for j in range(TT):
                if j == TT // 2:
                    pe.wait_ge(placed, 3)
                last = pe.matmul(u_ps[:, 0, 0:3 * TILES], place[:, j, :],
                                 marks[:, j].rearrange("p k s -> p (k s)"), start=(j == 0), stop=(j == TT - 1))
            last.then_inc(inverted, 1)
            pe.wait_ge(routed, 1)

            def expert(it, s):
                at = tile_at(it, s)
                column = tile_expert_i[0:1, at:at + 1] if it is None else tile_expert_i[0:1, bass.ds(at, 1)]
                return pe.value_load(column, min_val=0, max_val=E - 1)

            def part(s, it):
                if inside(it, s + 1):
                    wait_dma(pe, gathered, it, s + 1)
                    wait_n(pe, xT_ready, it, s)
                    for c in range(C):
                        last = pe.transpose(x_ps[:, c * P:(c + 1) * P], xg[:, (s + 1) % PERIOD, c * P:(c + 1) * P],
                                            ident[:])
                    last.then_inc(xT_psum, 1)
                if inside(it, s):
                    e = expert(it, s)
                    pe.wait_ge(experts_ready, e + 1)
                    wait_n(pe, xT_ready, it, s)
                    wait_n(pe, gate_act, it, s - 1)
                    for half in range(2):
                        for c in range(C):
                            last = pe.matmul(g_ps[:, half, 0:HALF], xT[:, s % 2, c, :],
                                             wg[:, bass.ds(e, 1), c, half * HALF:(half + 1) * HALF],
                                             start=(c == 0), stop=(c == C - 1))
                    last.then_inc(gate_ready, 1)
                if inside(it, s - 1):
                    wait_n(pe, h_ready, it, s - 1)
                    wait_n(pe, hT_low, it, s - 2)
                    wait_n(pe, hT_high, it, s - 2)
                    for k in range(HC):
                        n = P if k < HC - 1 else LAST
                        last = pe.transpose(t_ps[0:n, k // 4, (k % 4) * P:(k % 4 + 1) * P],
                                            h[:, (s - 1) % 2, k * P:k * P + n], ident[:])
                        if k == 3:
                            last.then_inc(hT_psum, 1)
                    last.then_inc(hT_psum, 1)
                if inside(it, s):
                    for half in range(2):
                        for c in range(C):
                            last = pe.matmul(u_ps[:, half, 0:HALF], xT[:, s % 2, c, :],
                                             wu[:, bass.ds(e, 1), c, half * HALF:(half + 1) * HALF],
                                             start=(c == 0), stop=(c == C - 1))
                    last.then_inc(up_ready, 1)
                if inside(it, s - 1):
                    e = expert(it, s - 1)
                    wait_n(pe, hT_low, it, s - 1)
                    wait_n(pe, hT_high, it, s - 1)
                    wait_n(pe, summed, it, s - 2)
                    for k in range(HC):
                        n = P if k < HC - 1 else LAST
                        last = pe.matmul(d_ps[:, 0:D], hT[0:n, (s - 1) % 2, k, :], wd[0:n, bass.ds(e, 1), k, :],
                                         start=(k == 0), stop=(k == HC - 1))
                    last.then_inc(down_ready, 1)

            run_slots(pe, part)

        @block.scalar
        def _(act):
            def part(s, it):
                if inside(it, s + 1):
                    wait_n(act, xT_psum, it, s + 1)
                    wait_n(act, up_ready, it, s - 1)
                    act.activation(xT[:, (s + 1) % 2].rearrange("p c t -> p (c t)"), x_ps[:, 0:C * P], ACT.Copy)\
                       .then_inc(xT_ready, 1)
                if inside(it, s):
                    wait_n(act, gate_ready, it, s)
                    wait_n(act, h_ready, it, s - 2)
                    act.activation(act_g[:, s % 2].rearrange("p (a n) -> p a n", a=2), halves(g_ps), ACT.Silu)\
                       .then_inc(gate_act, 1)
                if inside(it, s - 1):
                    wait_n(act, hT_psum, it, s - 1, 1, 2)
                    wait_n(act, down_ready, it, s - 3)
                    act.activation(hT[:, (s - 1) % 2, 0:4].rearrange("p k t -> p (k t)"), t_ps[:, 0, :], ACT.Copy)\
                       .then_inc(hT_low, 1)

            act.wait_ge(routed, 1)
            run_slots(act, part)

        @block.vector
        def _(dve):
            def one(n):
                dve.wait_ge(route_step, n)

            dve.wait_ge(consts, 3)
            dve.tensor_copy(iota_f[:], iota_i[:])
            dve.tensor_copy(iota_b[:], iota_i[:])
            dve.tensor_copy(row_f[:], row_i[:])
            dve.reduce_max(best[:], logits, axis=AX.X).then_inc(route_step, 1)
            one(1)
            per_expert = [P, TT, E]
            dve.tensor_tensor(pick[:], logits, best[:].unsqueeze(2).to_broadcast(per_expert), ALU.is_ge)\
               .then_inc(route_step, 1)
            one(2)
            dve.tensor_tensor(pick[:], pick[:], descend[:].unsqueeze(1).to_broadcast(per_expert), ALU.mult)\
               .then_inc(route_step, 1)
            one(3)
            dve.reduce_max(best[:], pick[:], axis=AX.X).then_inc(route_step, 1)
            one(4)
            dve.tensor_tensor(onehot[:], pick[:], best[:].unsqueeze(2).to_broadcast(per_expert), ALU.is_equal)\
               .then_inc(placed, 1)
            dve.wait_ge(ranked, 1)
            dve.reduce_sum(count[:], g_ps[:, 1, 0:TT * E].rearrange("p (j e) -> p e j", e=E), axis=AX.X)\
               .then_inc(route_step, 1)
            one(5)
            dve.tensor_scalar(count_i[:], count[:], float(P - 1), None, ALU.add).then_inc(route_step, 1)
            one(6)
            dve.tensor_scalar(count_i[:], count_i[:], SHIFT, None, ALU.arith_shift_right).then_inc(route_step, 1)
            one(7)
            dve.tensor_copy(ntiles[:], count_i[:]).then_inc(route_step, 1)
            one(8)
            dve.tensor_tensor(running[:], upto[:], ntiles[:].unsqueeze(1).to_broadcast([P, E, E]), ALU.mult)\
               .then_inc(route_step, 1)
            one(9)
            dve.reduce_sum(ends[:], running[:], axis=AX.X).then_inc(route_step, 1)
            one(10)
            dve.tensor_tensor(starts[:], ends[:], ntiles[:], ALU.subtract).then_inc(route_step, 1)
            one(11)
            dve.tensor_scalar(starts[:], starts[:], float(P), None, ALU.mult).then_inc(route_step, 1)
            one(12)
            dve.tensor_tensor(pick[:], g_ps[:, 0, 0:TT * E].rearrange("p (j e) -> p j e", e=E),
                              starts[:].unsqueeze(1).to_broadcast(per_expert), ALU.add).then_inc(route_step, 1)
            one(13)
            dve.tensor_tensor(pick[:], pick[:], onehot[:], ALU.mult).then_inc(route_step, 1)
            one(14)
            dve.reduce_sum(slot[:], pick[:], axis=AX.X).then_inc(route_step, 1)
            one(15)
            dve.tensor_copy(slot_i[:, 0, :], slot[:]).then_inc(route_step, 1)
            one(16)
            dve.tensor_scalar(slot_i[:, 1, :], slot_i[:, 0, :], SHIFT, None, ALU.arith_shift_right)
            dve.tensor_scalar(slot_i[:, 2, :], slot_i[:, 0, :], P - 1, None, ALU.bitwise_and).then_inc(route_step, 1)
            one(17)
            dve.tensor_copy(slot_b[:], slot_i[:, 1:3, :]).then_inc(route_step, 1)
            one(18)
            spread = [P, TT, TILES]
            dve.tensor_tensor(marks[:, :, 2, :], iota_b[:, 0:TILES].unsqueeze(1).to_broadcast(spread),
                              slot_b[:, 0, :].unsqueeze(2).to_broadcast(spread), ALU.is_equal)\
               .then_inc(route_step, 1)
            one(19)
            dve.tensor_tensor(marks[:, :, 0, :], marks[:, :, 2, :],
                              iota_b[:, 0:TT].unsqueeze(2).to_broadcast(spread), ALU.mult)
            dve.tensor_scalar(marks[:, :, 1, :], marks[:, :, 2, :], row_f[:], None, ALU.mult)
            some = [P, TT // 2, P]
            for j in (0, TT // 2):
                dve.tensor_tensor(place[:, j:j + TT // 2], iota_b[:].unsqueeze(1).to_broadcast(some),
                                  slot_b[:, 1, j:j + TT // 2].unsqueeze(2).to_broadcast(some), ALU.is_equal)\
                   .then_inc(placed, 1)
            dve.tensor_tensor(behind[:], ends[:].unsqueeze(1).to_broadcast([P, TILES, E]),
                              iota_f[:, 0:TILES].unsqueeze(2).to_broadcast([P, TILES, E]), ALU.is_le)\
               .then_inc(route_step, 1)
            one(20)
            dve.reduce_sum(tile_expert[:], behind[:], axis=AX.X).then_inc(route_step, 1)
            one(21)
            dve.tensor_scalar(tile_expert_i[:], tile_expert[:], float(E - 1), None, ALU.min)
            dve.wait_ge(inverted, 1)
            dve.tensor_copy(found[:].rearrange("p k s -> p (k s)"), u_ps[:, 0, 0:3 * TILES]).then_inc(route_step, 1)
            one(22)
            dve.scalar_tensor_tensor(take_f[:, 0, :], found[:, 0, :], float(P), found[:, 1, :], ALU.mult, ALU.add)
            dve.tensor_scalar(take_f[:, 1, :], found[:, 2, :], -SKIP, SKIP, ALU.mult, ALU.add).then_inc(route_step, 1)
            one(23)
            dve.tensor_tensor(take_f[:, 1, :], take_f[:, 1, :], take_f[:, 0, :], ALU.add).then_inc(route_step, 1)
            one(24)
            dve.tensor_copy(take[:], take_f[:]).then_inc(routed, 1)

            def own(it, s, n, alone=False):
                wait_n(dve, norm_step, it, s, n, NORM, alone)

            def part(s, it):
                if inside(it, s - 1):
                    wait_n(dve, hT_psum, it, s - 1, 2, 2)
                    wait_n(dve, down_ready, it, s - 3)
                    high = hT[:, (s - 1) % 2, 4:HC - 1].rearrange("p k t -> p (k t)")
                    dve.tensor_copy(high, t_ps[:, 1, 0:(HC - 5) * P])
                    dve.tensor_copy(hT[0:LAST, (s - 1) % 2, HC - 1, :], t_ps[0:LAST, 1, (HC - 5) * P:(HC - 4) * P])\
                       .then_inc(hT_high, 1)
                if inside(it, s):
                    wait_n(dve, up_ready, it, s)
                    wait_n(dve, gate_act, it, s)
                    wait_n(dve, hT_psum, it, s - 2, 2, 2)
                    dve.tensor_tensor(h[:, s % 2].rearrange("p (a n) -> p a n", a=2), halves(u_ps),
                                      act_g[:, s % 2].rearrange("p (a n) -> p a n", a=2), ALU.mult)\
                       .then_inc(h_ready, 1)
                if inside(it, s - 1):
                    t = s - 1
                    out_y = y[:, t % PERIOD, :]
                    wait_n(dve, down_ready, it, t)
                    wait_dma(dve, scattered, it, t - PERIOD)
                    dve.tensor_tensor(out_y, d_ps[:, 0:D], xg[:, t % PERIOD, :], ALU.add).then_inc(summed, 1)
                    wait_n(dve, summed, it, t)
                    var, root, scratch = rs[:, 0:1], rs[:, 1:2], rs[:, 2:3]
                    dve.bn_stats(stats[:], out_y).then_inc(norm_step, 1)
                    own(it, t, 1, alone=True)
                    dve.bn_aggr(moments[:], stats[:]).then_inc(norm_step, 1)
                    own(it, t, 2)
                    dve.tensor_scalar(var, moments[:, 1:2], EPS, None, ALU.add).then_inc(norm_step, 1)
                    own(it, t, 3)
                    dve.tensor_scalar(scratch.bitcast(I32), var.bitcast(I32), 1, None, ALU.arith_shift_right)\
                       .then_inc(norm_step, 1)
                    own(it, t, 4)
                    dve.tensor_scalar(root.bitcast(I32), scratch.bitcast(I32), -1.0, float(0x5F3759DF),
                                      ALU.mult, ALU.add).then_inc(norm_step, 1)
                    for n in range(NEWTON):
                        own(it, t, 5 + 3 * n)
                        dve.tensor_tensor(scratch, root, root, ALU.mult).then_inc(norm_step, 1)
                        own(it, t, 6 + 3 * n)
                        dve.scalar_tensor_tensor(scratch, scratch, -0.5, var, ALU.mult, ALU.mult)\
                           .then_inc(norm_step, 1)
                        own(it, t, 7 + 3 * n)
                        dve.scalar_tensor_tensor(root, scratch, 1.5, root, ALU.add, ALU.mult)\
                           .then_inc(norm_step, 1)
                    own(it, t, NORM)
                    dve.tensor_scalar(out_y, out_y, moments[:, 0:1], root, ALU.subtract, ALU.mult)\
                       .then_inc(y_ready, 1)

            run_slots(dve, part)

        @block.gpsimd
        def _(pool):
            pool.memset(ident[:], 0.0)
            pool.memset(before[:], 1.0)
            pool.memset(ones[:], 1.0)
            pool.memset(upto[:], 1.0)
            pool.iota(iota_i[:], pattern=[[1, P]], base=0, channel_multiplier=0)
            for e in range(E):
                last = pool.memset(descend[:, e:e + 1], float(E - e))
            pool.iota(row_i[:], pattern=[[0, 1]], base=0, channel_multiplier=1).then_inc(consts, 1)
            pool.wait_ge(consts, 1)
            pool.affine_select(out=ident[:], in_=ident[:], compare_op=ALU.not_equal, fill=1.0, base=0,
                               pattern=[[-1, P]], channel_multiplier=1)
            pool.affine_select(out=before[:], in_=before[:], compare_op=ALU.is_ge, fill=0.0, base=-1,
                               pattern=[[1, P]], channel_multiplier=-1)
            pool.affine_select(out=upto[:], in_=upto[:], compare_op=ALU.is_ge, fill=0.0, base=0,
                               pattern=[[1, E], [-1, E]], channel_multiplier=0).then_inc(consts, 2)
            pool.wait_ge(routed, 1)

            def part(s, it):
                if inside(it, s + 3):
                    t = s + 3
                    wait_dma(pool, gathered, it, t - 2)
                    at = tile_at(it, t)
                    column = take[:, 0, at:at + 1] if it is None else take[:, 0, bass.ds(at, 1)]
                    pool.tensor_copy(now[:, 0, t % 2:t % 2 + 1], column).then_inc(index_copied, 1)
                    wait_index(it, s, 0)
                    wait_n(pool, summed, it, t - PERIOD)
                    pool.indirect_dma_start(out=xg[:, t % PERIOD, :], out_offset=None, in_=x2,
                                            in_offset=bass.IndirectOffsetOnAxis(ap=now[:, 0, t % 2:t % 2 + 1], axis=0),
                                            bounds_check=TOKENS - 1, oob_is_err=False)\
                        .then_inc(gathered[t % PERIOD], 16)
                if inside(it, s - 2):
                    t = s - 2
                    wait_dma(pool, scattered, it, t - 2)
                    at = tile_at(it, t)
                    column = take[:, 1, at:at + 1] if it is None else take[:, 1, bass.ds(at, 1)]
                    pool.tensor_copy(now[:, 1, t % 2:t % 2 + 1], column).then_inc(index_copied, 1)
                    wait_index(it, s, 1)
                    wait_n(pool, y_ready, it, t)
                    pool.indirect_dma_start(out=out,
                                            out_offset=bass.IndirectOffsetOnAxis(ap=now[:, 1, t % 2:t % 2 + 1], axis=0),
                                            in_=y[:, t % PERIOD, :], in_offset=None,
                                            bounds_check=TOKENS - 1, oob_is_err=False)\
                        .then_inc(scattered[t % PERIOD], 16)

            def wait_index(it, s, n):
                copies = min(s + 4, TILES) + max(0, s - 2) + n * (s >= 2)
                if it is None:
                    pool.wait_ge(index_copied, copies)
                else:
                    wait_count(pool, index_copied, it * (2 * PERIOD) + (s + 4 + s - 2 + n))

            run_slots(pool, part)
            for n in range(PERIOD):
                pool.wait_ge(scattered[n], 16 * len(range(n, TILES, PERIOD)))

        @block.sync
        def _(sp):
            for e in range(E):
                sp.dma_start(wg[:, e], gate_w[e].rearrange("(c p) i -> p c i", p=P)).then_inc(expert_loaded[e], 16)
                sp.dma_start(wu[:, e], up_w[e].rearrange("(c p) i -> p c i", p=P)).then_inc(expert_loaded[e], 16)
                sp.dma_start(wd[:, e, 0:HC - 1], down_w[e, 0:(HC - 1) * P, :].rearrange("(k p) d -> p k d", p=P))\
                  .then_inc(expert_loaded[e], 16)
                sp.dma_start(wd[0:LAST, e, HC - 1], down_w[e, (HC - 1) * P:HID, :]).then_inc(expert_loaded[e], 16)
            for e in range(E):
                sp.wait_ge(expert_loaded[e], 64)
                sp.sem_inc(experts_ready, 1)


def build(nc, a, out):
    x1 = nc.dram_tensor("x1_dram", [TOKENS, D], FP32, kind="Internal").ap()
    x2 = nc.dram_tensor("x2_dram", [TOKENS, D], FP32, kind="Internal").ap()
    with nc.sbuf_tensor("logits", [P, BATCH * T, EXPERTS], FP32) as logits:
        with ExitStack() as ctx:
            bufs = attention_buffers(nc, ctx)
            cross_weights = a["xwq"], a["xwkv"], a["xwo"]
            attention_phase(nc, False, bufs, a["x"], a["xT"], (a["wq"], a["wkv"], a["wo"]), x1,
                            after=(*cross_weights, a["mask"], a["rope"], a["router"]))
            attention_phase(nc, True, bufs, x1, a["ctxT"], cross_weights, x2, logits=logits[:])
        expert_phase(nc, x2, logits[:], a["gate_w"], a["up_w"], a["down_w"], out)


def rotary_tables():
    half = DH // 2
    exps = np.arange(1, DH + 1, 2, dtype=np.float32)[:half] / np.float32(DH)
    w = np.float32(1.0) / np.float32(10000.0) ** exps
    angles = np.arange(1, SEQ + 1, dtype=np.float32)[:, None] * w[None, :]
    cos = np.repeat(np.cos(angles), 2, axis=1)
    sin = np.stack([-np.sin(angles), np.sin(angles)], axis=-1).reshape(SEQ, DH)
    both = np.stack([cos, sin]).reshape(2, T, P, DH)
    return np.ascontiguousarray(both.transpose(2, 0, 1, 3)).astype(np.float32)


def kernel(**inputs):
    from concourse import bacc
    from concourse.bass_utils import run_bass_kernel_spmd

    def arr(name):
        return np.asarray(inputs[name])

    def transposed(a):
        return np.ascontiguousarray(a.T)

    x = arr("x").reshape(TOKENS, D)
    arrays = {
        "x": x,
        "xT": transposed(x),
        "wq": transposed(arr("L0_attn_wq")),
        "wkv": np.concatenate([arr("L0_attn_wk").T, arr("L0_attn_wv").T], axis=1),
        "wo": transposed(arr("L0_attn_wo")),
        "ctxT": transposed(arr("ctx_1024").reshape(TOKENS, D)),
        "xwq": arr("L0_xattn_W_q"),
        "xwkv": arr("L0_xattn_W_kv"),
        "xwo": arr("L0_xattn_W_c"),
        "mask": transposed(arr("mask_BxS2_bf1").reshape(BATCH * T, P)).view(np.uint8),
        "rope": rotary_tables(),
        "router": transposed(arr("L0_ffn_router_w")),
        "gate_w": arr("L0_ffn_gate_w").transpose(0, 2, 1),
        "up_w": arr("L0_ffn_up_w").transpose(0, 2, 1),
        "down_w": arr("L0_ffn_down_w").transpose(0, 2, 1),
    }
    arrays = {n: np.ascontiguousarray(v) for n, v in arrays.items()}
    nc = bacc.Bacc("TRN2", target_bir_lowering=False, num_devices=1, dynamic_dma_scratch_size=8192)
    a = {n: nc.dram_tensor(f"in_{n}", list(v.shape), mybir.dt.from_np(v.dtype), kind="ExternalInput").ap()
         for n, v in arrays.items()}
    out = nc.dram_tensor("out_dram", [TOKENS, D], FP32, kind="ExternalOutput").ap()
    build(nc, a, out)
    r = run_bass_kernel_spmd(nc, [{f"in_{n}": v for n, v in arrays.items()}], core_ids=[0])
    return r.results[0]["out_dram"].reshape(BATCH, SEQ, D)
```
